# Optimizing a Trainium2 kernel written in Bass

```python
import numpy as np
import jax
import jax.numpy as jnp

def _softmax(x, axis=-1):
    return jax.nn.softmax(x, axis=axis)

def _gelu(x):
    return jax.nn.gelu(x, approximate=True)

def _silu(x):
    return jax.nn.silu(x)

def _sigmoid(x):
    return jax.nn.sigmoid(x)

def _layernorm(x, axis=-1, eps=1e-05):
    m = jnp.mean(x, axis=axis, keepdims=True)
    v = jnp.var(x, axis=axis, keepdims=True)
    return (x - m) / jnp.sqrt(v + eps)

def _scatter_add(tgt, idx, src, axis=0):
    return tgt.at[idx].add(src)

def _segment_sum(src, seg, n):
    return jax.ops.segment_sum(src, seg, n)
kernel_name = 'mk_xattn_seq_d1_seqx_r2_7c8501'

def setup_inputs(seed: int=0):
    np.random.seed(seed)
    _w = jnp.asarray

    def _rec_inputs():
        import jax
        import jax.numpy as jnp
        _rk = jax.random.key(seed)
        x = -0.0002928 + 1 * jax.random.normal(jax.random.fold_in(_rk, 1), (8, 512, 1024), jnp.float32)
        _lenS = 512 - jax.random.randint(jax.random.fold_in(_rk, 7), (8,), 0, max(1, 512 // 4) + 1, jnp.int32)
        _lenS2 = 512 - jax.random.randint(jax.random.fold_in(_rk, 8), (8,), 0, max(1, 512 // 4) + 1, jnp.int32)
        _ctx_2048P = jax.random.normal(jax.random.fold_in(_rk, 12), (8, 16, 1024), jnp.float32)
        _ctx_2048c = jax.random.dirichlet(jax.random.fold_in(_rk, 512), 0.3 * jnp.ones((16,), jnp.float32), (8, 512))
        _ctx_2048t = jnp.einsum('bsk,bkd->bsd', _ctx_2048c, _ctx_2048P)
        _ctx_2048t = _ctx_2048t * jax.lax.rsqrt(jnp.mean(jnp.square(_ctx_2048t)) + 1e-12) * 0.953939
        ctx_2048 = -1.39393e-06 + 0.999914 * (_ctx_2048t + 0.3 * jax.random.normal(jax.random.fold_in(_rk, 612), (8, 512, 1024), jnp.float32))
        _validS = jnp.arange(512)[None, :] < _lenS[:, None]
        _validS2 = jnp.arange(512)[None, :] < _lenS2[:, None]
        _causal = jnp.tril(jnp.ones((512, 512), dtype=bool))
        mask_Bx1x2048_bf1 = jnp.ones((8, 1, 1024), dtype=bool)
        return (x, ctx_2048, mask_Bx1x2048_bf1)
    x, ctx_2048, mask_Bx1x2048_bf1 = _rec_inputs()

    def _L0_xattn_setup():
        import jax, jax.numpy as jnp
        import numpy as np
        import math
        N_HEADS = 16
        EPS = 1e-05

        def _masked_instance_norm(x, mask):
            m = mask.astype(x.dtype)
            x = x * m
            n_valid = jnp.sum(m, axis=-1, keepdims=True)
            mean = jnp.sum(x, axis=-1, keepdims=True) / n_valid
            var = jnp.sum(x * x, axis=-1, keepdims=True) / n_valid - mean * mean
            x = (x - mean) / jnp.sqrt(jax.nn.relu(var) + EPS)
            return x * m
        key = jax.random.key(seed)
        ks = jax.random.split(key, 8)
        bs, c, t1, t2 = (2, 512, 1024, 1024)
        s = 1.0 / math.sqrt(c)
        return {'x': jax.random.normal(ks[0], (bs, c, t1), jnp.float32), 'mask': jnp.ones((bs, 1, t1), jnp.bool_), 'kv': jax.random.normal(ks[1], (bs, c, t2), jnp.float32), 'kv_mask': jnp.ones((bs, 1, t2), jnp.bool_), 'Wq': jax.random.normal(ks[2], (c, c), jnp.float32) * s, 'bq': jnp.zeros((c,), jnp.float32), 'Wk': jax.random.normal(ks[3], (c, c), jnp.float32) * s, 'bk': jnp.zeros((c,), jnp.float32), 'Wv': jax.random.normal(ks[4], (c, c), jnp.float32) * s, 'bv': jnp.zeros((c,), jnp.float32)}
    _L0_xattn_all = _L0_xattn_setup()
    _L0_xattn_in = {k: v for k, v in _L0_xattn_all.items() if k in ('Wq', 'bq', 'Wk', 'bk', 'Wv', 'bv')}
    del _L0_xattn_all
    return {'x': x, 'ctx_2048': ctx_2048, 'mask_Bx1x2048_bf1': mask_Bx1x2048_bf1, 'L0_xattn_Wq': _L0_xattn_in['Wq'], 'L0_xattn_bq': _L0_xattn_in['bq'], 'L0_xattn_Wk': _L0_xattn_in['Wk'], 'L0_xattn_bk': _L0_xattn_in['bk'], 'L0_xattn_Wv': _L0_xattn_in['Wv'], 'L0_xattn_bv': _L0_xattn_in['bv']}

def reference(x, ctx_2048, mask_Bx1x2048_bf1, L0_xattn_Wq, L0_xattn_bq, L0_xattn_Wk, L0_xattn_bk, L0_xattn_Wv, L0_xattn_bv):
    import jax
    import jax.numpy as jnp

    def _L0_xattn_ref(x, mask, kv, kv_mask, Wq, bq, Wk, bk, Wv, bv):
        import jax, jax.numpy as jnp
        import numpy as np
        import math
        N_HEADS = 16
        EPS = 1e-05

        def _masked_instance_norm(x, mask):
            m = mask.astype(x.dtype)
            x = x * m
            n_valid = jnp.sum(m, axis=-1, keepdims=True)
            mean = jnp.sum(x, axis=-1, keepdims=True) / n_valid
            var = jnp.sum(x * x, axis=-1, keepdims=True) / n_valid - mean * mean
            x = (x - mean) / jnp.sqrt(jax.nn.relu(var) + EPS)
            return x * m
        bs, c, t1 = x.shape
        h = N_HEADS
        d = c // h
        scale = 1.0 / math.sqrt(d)
        q = jnp.einsum('oc,bct->bot', Wq, x) + bq[None, :, None]
        k = jnp.einsum('oc,bct->bot', Wk, kv) + bk[None, :, None]
        v = jnp.einsum('oc,bct->bot', Wv, kv) + bv[None, :, None]
        q = q.reshape(bs, h, d, t1).transpose(0, 1, 3, 2)
        k = k.reshape(bs, h, d, -1)
        v = v.reshape(bs, h, d, -1).transpose(0, 1, 3, 2)
        attn = jnp.einsum('bhqd,bhdk->bhqk', q * scale, k)
        attn = jnp.where(kv_mask[:, :, None, :], attn, -jnp.inf)
        attn = jax.nn.softmax(attn, axis=-1)
        mean = jnp.einsum('bhqk,bhkd->bhqd', attn, v)
        ex2 = jnp.einsum('bhqk,bhkd->bhqd', attn, v * v)
        std = jnp.sqrt(jax.nn.relu(ex2 - mean * mean))
        mean = mean.transpose(0, 1, 3, 2).reshape(bs, c, t1)
        std = std.transpose(0, 1, 3, 2).reshape(bs, c, t1)
        xn = _masked_instance_norm(x, mask)
        out = (xn * std + mean) * mask.astype(x.dtype)
        return out
    x = _L0_xattn_ref(x, mask_Bx1x2048_bf1, ctx_2048, mask_Bx1x2048_bf1, L0_xattn_Wq, L0_xattn_bq, L0_xattn_Wk, L0_xattn_bk, L0_xattn_Wv, L0_xattn_bv)
    return x

_drawn_inputs = setup_inputs


def setup_inputs(seed=0):
    import zlib

    import numpy as np

    out = dict(_drawn_inputs(seed))
    spreads = {'L0_xattn_bq': (0.0, 0.281), 'L0_xattn_bk': (0.0, 0.8), 'L0_xattn_bv': (0.0, 0.1)}
    factors = {}
    for name, (base, spread) in spreads.items():
        noise = np.random.default_rng([zlib.crc32(name.encode()), seed]).standard_normal(out[name].shape)
        drawn = base * np.exp(spread * noise) if base else spread * noise
        out[name] = jnp.asarray(drawn.astype(out[name].dtype))
    for name, factor in factors.items():
        out[name] = (out[name] * factor).astype(out[name].dtype)
    return out
```

```python
from contextlib import ExitStack

import concourse.bass as bass
from concourse import mybir

F32 = mybir.dt.float32
F32R = mybir.dt.float32r
U8 = mybir.dt.uint8
ALU = mybir.AluOpType
ACT = mybir.ActivationFunctionType
AX_X = mybir.AxisListType.X

P = 128
EPS = 1e-5
MASKED = 2.0 ** 127


def wait(eng, sem, value):
    if isinstance(value, int) and value <= 0:
        return
    eng.wait_ge(sem, value)


def settled_wait(eng, sem, value):
    wait(eng, sem, value)
    if not isinstance(value, int):
        eng.nop(nofuse=True)


def project(nc, x, kv, mask, wqT, bq, wkT, bk, wvT, bv, scratch, norm_ab):
    B, C, T = x.shape
    CT = C // P
    TT = T // P
    HALF = 512
    NH = T // HALF
    HD = 32
    HEADS = C // HD
    BANKS = 8
    TILES = CT * NH
    TPB = 2 * TILES + TT
    assert TPB % BANKS == 0 and CT == 4 and NH == 2
    q_hi, q_lo, k_hi, k_lo, v_t, mask_f, mask_b = scratch

    with ExitStack() as ctx:
        def sb(name, shape, dt):
            return ctx.enter_context(nc.sbuf_tensor(name, shape, dt))

        def sem(name):
            return ctx.enter_context(nc.semaphore(name))

        w_hi = sb("w_hi", [P, 3, CT, C], F32R)
        w_lo = sb("w_lo", [P, 3, CT, C], F32R)
        raw = sb("raw", [P, 4, T], F32)
        in_hi = sb("in_hi", [P, 2 * CT, T], F32R)
        in_lo = sb("in_lo", [P, 2 * CT, T], F32R)
        out_hi = sb("out_hi", [P, 2, T], F32R)
        out_lo = sb("out_lo", [P, 2, T], F32R)
        v_sb = sb("v_sb", [P, HEADS, TT, HD], F32)
        xm = sb("xm", [P, T], F32)
        junk = sb("junk", [P, T], F32)
        mask_u8 = sb("mask_u8", [P, T], U8)
        mask_sb = sb("mask_sb", [P, T], F32)
        mask_row = sb("mask_row", [1, T], F32)
        bqk = sb("bqk", [P, 2, CT], F32)
        bv_sb = sb("bv_sb", [P, C], F32)
        sum4 = sb("sum4", [P, CT], F32)
        sq4 = sb("sq4", [P, CT], F32)
        sums = sb("sums", [P, B * CT], F32)
        sqs = sb("sqs", [P, B * CT], F32)
        nval = sb("nval", [P, B], F32)
        rn = sb("rn", [P, B], F32)
        mean = sb("mean", [P, B * CT], F32)
        mean2 = sb("mean2", [P, B * CT], F32)
        var = sb("var", [P, B * CT], F32)
        ps = [ctx.enter_context(nc.psum_tensor(f"proj{i}", [P, HALF], F32)) for i in range(BANKS)]

        w_in = [sem(f"w_in{i}") for i in range(3)]
        w_hi_done = sem("w_hi_done")
        w_lo_done = sem("w_lo_done")
        consts_in = sem("consts_in")
        raw_in = [sem(f"raw_in{i}") for i in range(4)]
        mask_in = sem("mask_in")
        hi_done = sem("hi_done")
        lo_done = sem("lo_done")
        mask_done = sem("mask_done")
        maskrow_done = sem("maskrow_done")
        nval_done = sem("nval_done")
        xm_done = sem("xm_done")
        sq_done = sem("sq_done")
        stat_done = sem("stat_done")
        mm_done = sem("mm_done")
        outhi_done = sem("outhi_done")
        evac_done = sem("evac_done")
        stored = [sem(f"stored{i}") for i in range(2)]
        v_stored = sem("v_stored")
        mask_stored = sem("mask_stored")
        chain = sem("chain")
        root = sem("root")

        block = ctx.enter_context(nc.Block())

        def over_batches(eng, body):
            body(0)
            with eng.Fori(1, B - 1) as b:
                body(b)
            body(B - 1, last=True)

        @block.sync
        def _(sp):
            def load_w(j, w):
                if j == 2:
                    sp.wait_ge(w_lo_done, 1)
                half = raw[:, 2 * (j % 2):2 * (j % 2) + 2, :].rearrange("p s (c o) -> p (s c) o", o=C)
                sp.dma_start(half, w.rearrange("(c p) o -> p c o", p=P)).then_inc(w_in[j], 16)

            load_w(0, wqT)
            load_w(1, wkT)
            load_w(2, wvT)
            sp.dma_start(bqk[:, 0, :], bq).then_inc(consts_in, 16)
            sp.dma_start(bqk[:, 1, :], bk).then_inc(consts_in, 16)
            sp.dma_start(bv_sb[:, :], bv.rearrange("(a o) -> a o", a=1).broadcast_to([P, C])).then_inc(consts_in, 16)

            def load_inputs(b, src, first):
                for r in range(CT):
                    if first == 0:
                        if isinstance(b, int) and b == 0:
                            sp.wait_ge(w_lo_done, 3 if r < 2 else 2)
                        else:
                            sp.wait_ge(lo_done, 8 * b - 3 + r)
                    else:
                        settled_wait(sp, lo_done, 8 * b + 1 + r)
                        sp.wait_ge(xm_done, 4 * b + 1 + r)
                    sp.dma_start(raw[:, r, :], src[b, r * P:(r + 1) * P, :] if isinstance(b, int)
                                 else src[bass.ds(b, 1), r * P:(r + 1) * P, :].rearrange("a p t -> (a p) t")
                                 ).then_inc(raw_in[r], 16)

            def load_mask(b):
                settled_wait(sp, mask_done, b)
                row = mask[b] if isinstance(b, int) else mask[bass.ds(b, 1)].rearrange("a o t -> (a o) t")
                sp.dma_start(mask_u8[:, :], row.broadcast_to([P, T])).then_inc(mask_in, 16)

            def store_masks(b):
                sp.wait_ge(maskrow_done, b + 1)
                for g in range(CT):
                    sp.dma_start(mask_f[bass.ds(b * CT + g, 1), :], mask_sb[0:1, :]).then_inc(mask_stored, 16)
                    sp.dma_start(mask_b[bass.ds(b * CT + g, 1), :], mask_row[:, :]).then_inc(mask_stored, 16)

            load_mask(0)
            load_inputs(0, x, 0)
            store_masks(0)
            load_inputs(0, kv, 4)

            def body(b, last=False):
                if not last:
                    load_mask(b + 1)
                    load_inputs(b + 1, x, 0)

                def store(n, hi, lo):
                    for o in range(CT):
                        sp.wait_ge(evac_done, TPB * b + 2 * (n + o) + 2)
                        rows = bass.ds(b * C + o * P, P)
                        sp.dma_start(hi[rows, :], out_hi[:, o % 2, :].bitcast(F32)).then_inc(stored[o % 2], 16)
                        sp.dma_start(lo[rows, :], out_lo[:, o % 2, :].bitcast(F32)).then_inc(stored[o % 2], 16)

                store(0, q_hi, q_lo)
                if not last:
                    store_masks(b + 1)
                    load_inputs(b + 1, kv, 4)
                store(4, k_hi, k_lo)
                sp.wait_ge(evac_done, TPB * b + TPB)
                for g in range(CT):
                    sp.dma_start(v_t[bass.ds(b * C + g * P, P), :],
                                 v_sb[:, 4 * g:4 * g + 4, :, :].rearrange("p h t d -> p (h t d)")
                                 ).then_inc(v_stored, 16)

            over_batches(sp, body)
            for s in stored:
                sp.wait_ge(s, B * 4 * 32)
            sp.wait_ge(v_stored, B * CT * 16)
            sp.wait_ge(mask_stored, B * CT * 32)

        @block.scalar
        def _(act):
            for j in range(3):
                act.wait_ge(w_in[j], 16)
                half = raw[:, 2 * (j % 2):2 * (j % 2) + 2, :].rearrange("p s (c o) -> p (s c) o", o=C)
                act.activation(w_hi[:, j, :, :], half, ACT.Copy).then_inc(w_hi_done, 1)

            def split(b, first):
                for r in range(CT):
                    wait(act, mm_done, TPB * b - TPB + TILES if first == 0 else TPB * b)
                    act.wait_ge(raw_in[r], 32 * b + (16 if first == 0 else 32))
                    act.activation(in_hi[:, first + r, :], raw[:, r, :], ACT.Copy).then_inc(hi_done, 1)
                    if first == 0:
                        act.wait_ge(xm_done, 4 * b + r + 1)
                        wait(act, sq_done, 4 * b + r)
                        if r == 0:
                            wait(act, stat_done, 2 * b)
                        act.activation(junk[:, :], xm[:, :], ACT.Square,
                                       accum_out=sq4[:, r:r + 1]).then_inc(sq_done, 1)

            def evacuate_hi(b, n):
                for i in range(TILES):
                    o, half = i // NH, i % NH
                    t = TILES * n + i
                    act.wait_ge(mm_done, TPB * b + t + 1)
                    if half == 0:
                        wait(act, stored[o % 2], 32 * (4 * b + 2 * n + o // 2))
                    act.activation(out_hi[:, o % 2, half * HALF:(half + 1) * HALF], ps[t % BANKS][:, :],
                                   ACT.Identity, bias=bqk[:, n, o:o + 1]).then_inc(outhi_done, 1)

            act.wait_ge(consts_in, 48)
            split(0, 0)
            split(0, 4)

            def body(b, last=False):
                evacuate_hi(b, 0)
                if not last:
                    split(b + 1, 0)
                evacuate_hi(b, 1)
                if not last:
                    split(b + 1, 4)

            over_batches(act, body)
            act.wait_ge(chain, 5)
            act.activation(mean2[:, :], var[:, :], ACT.Sqrt).then_inc(root, 1)

        @block.vector
        def _(dve):
            for j in range(3):
                dve.wait_ge(w_hi_done, j + 1)
                half = raw[:, 2 * (j % 2):2 * (j % 2) + 2, :].rearrange("p s (c o) -> p (s c) o", o=C)
                dve.tensor_tensor(w_lo[:, j, :, :], half, w_hi[:, j, :, :].bitcast(F32),
                                  ALU.subtract).then_inc(w_lo_done, 1)

            def take_mask(b):
                settled_wait(dve, mask_in, 16 * b + 16)
                settled_wait(dve, mask_stored, 32 * CT * b)
                wait(dve, xm_done, 4 * b)
                dve.tensor_copy(mask_sb[:, :], mask_u8[:, :]).then_inc(mask_done, 1)
                dve.wait_ge(mask_done, b + 1)
                dve.tensor_scalar(mask_row[:, :], mask_sb[0:1, :], MASKED, -MASKED, ALU.mult,
                                  ALU.add).then_inc(maskrow_done, 1)
                dve.tensor_reduce(nval[:, bass.ds(b, 1)], mask_sb[:, :], AX_X, ALU.add).then_inc(nval_done, 1)

            def split(b, first):
                if first == 0:
                    take_mask(b)
                for r in range(CT):
                    dve.wait_ge(hi_done, 8 * b + first + r + 1)
                    wait(dve, mm_done, TPB * b - TPB + TILES if first == 0 else TPB * b)
                    dve.tensor_tensor(in_lo[:, first + r, :], raw[:, r, :], in_hi[:, first + r, :].bitcast(F32),
                                      ALU.subtract).then_inc(lo_done, 1)
                    if first == 0:
                        settled_wait(dve, sq_done, 4 * b + r)
                        if r == 0:
                            wait(dve, stat_done, 2 * b)
                        wait(dve, xm_done, 4 * b + r)
                        dve.tensor_tensor_reduce(xm[:, :], raw[:, r, :], mask_sb[:, :], 1.0, 0.0, ALU.mult,
                                                 ALU.add, sum4[:, r:r + 1]).then_inc(xm_done, 1)
                if first == 0:
                    dve.wait_ge(xm_done, 4 * b + 4)
                    dve.tensor_copy(sums[:, bass.ds(b * CT, CT)], sum4[:, :]).then_inc(stat_done, 1)
                    settled_wait(dve, sq_done, 4 * b + 4)
                    dve.tensor_copy(sqs[:, bass.ds(b * CT, CT)], sq4[:, :]).then_inc(stat_done, 1)

            def evacuate_lo(b, n):
                for i in range(TILES):
                    o, half = i // NH, i % NH
                    t = TILES * n + i
                    dve.wait_ge(outhi_done, 2 * TILES * b + t + 1)
                    if half == 0:
                        wait(dve, stored[o % 2], 32 * (4 * b + 2 * n + o // 2))
                    cols = slice(half * HALF, (half + 1) * HALF)
                    dve.scalar_tensor_tensor(out_lo[:, o % 2, cols], ps[t % BANKS][:, :], bqk[:, n, o:o + 1],
                                             out_hi[:, o % 2, cols].bitcast(F32), ALU.add,
                                             ALU.subtract).then_inc(evac_done, 1)

            def evacuate_v(b):
                for i in range(TT):
                    t = 2 * TILES + i
                    settled_wait(dve, mm_done, TPB * b + t + 1)
                    wait(dve, v_stored, 16 * CT * b)
                    dve.tensor_tensor(v_sb[:, :, i, :], ps[t % BANKS][:, :].rearrange("p (h d) -> p h d", d=HD),
                                      bv_sb[:, :].rearrange("p (h d) -> p h d", d=HD),
                                      ALU.add).then_inc(evac_done, 1)

            dve.wait_ge(consts_in, 48)
            split(0, 0)
            split(0, 4)

            def body(b, last=False):
                evacuate_lo(b, 0)
                if not last:
                    split(b + 1, 0)
                evacuate_lo(b, 1)
                evacuate_v(b)
                if not last:
                    split(b + 1, 4)

            over_batches(dve, body)

            dve.wait_ge(stat_done, 2 * B)
            dve.wait_ge(nval_done, B)
            dve.reciprocal(rn[:, :], nval[:, :]).then_inc(chain, 1)
            dve.wait_ge(chain, 1)
            by_batch = rn[:, :].rearrange("p (b o) -> p b o", o=1).broadcast_to([P, B, CT])

            def grouped(t):
                return t[:, :].rearrange("p (b c) -> p b c", c=CT)

            dve.tensor_tensor(grouped(mean), grouped(sums), by_batch, ALU.mult).then_inc(chain, 1)
            dve.tensor_tensor(grouped(var), grouped(sqs), by_batch, ALU.mult).then_inc(chain, 1)
            dve.wait_ge(chain, 3)
            dve.tensor_tensor(mean2[:, :], mean[:, :], mean[:, :], ALU.mult).then_inc(chain, 1)
            dve.wait_ge(chain, 4)
            dve.tensor_tensor(sqs[:, :], var[:, :], mean2[:, :], ALU.subtract).then_inc(root, 1)
            dve.wait_ge(root, 1)
            dve.tensor_scalar(var[:, :], sqs[:, :], 0.0, EPS, ALU.max, ALU.add).then_inc(chain, 1)
            dve.wait_ge(root, 2)
            dve.reciprocal(norm_ab[:, 0, :], mean2[:, :]).then_inc(chain, 1)
            dve.wait_ge(chain, 6)
            dve.scalar_tensor_tensor(norm_ab[:, 1, :], mean[:, :], -1.0, norm_ab[:, 0, :], ALU.mult,
                                     ALU.mult).then_inc(chain, 1)
            dve.wait_ge(chain, 7)

        @block.tensor
        def _(pe):
            pe.wait_ge(w_lo_done, 3)

            def products(b, t, pairs):
                wait(pe, evac_done, TPB * b + t - BANKS + 1)
                for n, (lhsT, rhs) in enumerate(pairs):
                    mm = pe.matmul(ps[t % BANKS][:, :], lhsT, rhs, start=(n == 0), stop=(n == len(pairs) - 1))
                mm.then_inc(mm_done, 1)

            def parts(a_hi, a_lo, b_hi, b_lo):
                return [(a_hi, b_hi), (a_hi, b_lo), (a_lo, b_hi)]

            def body(b, last=False):
                for n in range(2):
                    pe.wait_ge(lo_done, 8 * b + 4 + 4 * n)
                    for i in range(TILES):
                        out = slice((i // NH) * P, (i // NH + 1) * P)
                        cols = slice((i % NH) * HALF, (i % NH + 1) * HALF)
                        pairs = []
                        for c in range(CT):
                            pairs += parts(w_hi[:, n, c, out], w_lo[:, n, c, out],
                                           in_hi[:, 4 * n + c, cols], in_lo[:, 4 * n + c, cols])
                        products(b, TILES * n + i, pairs)
                for i in range(TT):
                    rows = slice(i * P, (i + 1) * P)
                    pairs = []
                    for c in range(CT):
                        pairs += parts(in_hi[:, 4 + c, rows], in_lo[:, 4 + c, rows],
                                       w_hi[:, 2, c, :], w_lo[:, 2, c, :])
                    products(b, 2 * TILES + i, pairs)

            over_batches(pe, body)


def attend(nc, x, out, ident_in, scratch, sum_rows, recip_rows, norm_ab):
    B, C, T = x.shape
    HD = 32
    GH = P // HD
    NG = B * C // P
    KT = T // P
    QH = 512
    SCALE = float(HD) ** -0.5
    MASK_ROW, MAX_ROW, ROWS = 3 * HD, 3 * HD + 1, 3 * HD + 3
    MACROS = 8
    assert GH == 4 and KT == 8 and T == 2 * QH
    q_hi, q_lo, k_hi, k_lo, v_t, mask_f, mask_b = scratch
    x_rows = x.rearrange("b c t -> (b c) t")
    out_rows = out.rearrange("b c t -> (b c) t")

    with ExitStack() as ctx:
        def sb(name, shape, dt):
            return ctx.enter_context(nc.sbuf_tensor(name, shape, dt))

        def psum(name, shape):
            return ctx.enter_context(nc.psum_tensor(name, shape, F32))

        def sem(name):
            return ctx.enter_context(nc.semaphore(name))

        q_sb = sb("q_sb", [P, GH, T], F32R)
        k_sb = sb("k_sb", [P, GH, T], F32R)
        v_sb = sb("v_sb_", [P, GH, KT * HD], F32)
        vv_sb = sb("vv_sb", [P, GH, KT, 2 * HD], F32)
        probs = sb("probs", [P, 4, KT, QH], F32)
        add_a = sb("add_a", [P, 2, 2 * QH], F32)
        add_b = sb("add_b", [P, 2, 2 * QH], F32)
        added = sb("added", [P, 2, GH, 2, QH], F32)
        pv_sb = sb("pv_sb", [P, 2, T], F32)
        mean_a = sb("mean_a", [P, T], F32)
        mean_b = sb("mean_b", [P, T], F32)
        sq_a = sb("sq_a", [P, T], F32)
        sq_b = sb("sq_b", [P, T], F32)
        mean = sb("mean_", [P, T], F32)
        msq = sb("msq", [P, T], F32)
        std = sb("std", [P, T], F32)
        x_sb = sb("x_sb", [P, T], F32)
        recip = sb("recip", [P, T], F32)
        sum_sb = sb("sum_sb", [P, T], F32)
        sum_c = sb("sum_c", [P, GH, T // P], F32)
        recip_c = sb("recip_c", [P, GH, T // P], F32)
        recip_m = sb("recip_m", [P, GH, T // P], F32)
        mask_c = sb("mask_c", [P, T // P], F32)
        negmax = sb("negmax", [P, KT], F32)
        negmax_parts = sb("negmax_parts", [P, 2 * KT], F32)
        negmax_rows = sb("negmax_rows", [2 * KT, P], F32R)
        ab = sb("ab", [P, 2], F32)
        ones = sb("ones", [P, HD], F32)
        ident = sb("ident", [P, P], F32)

        score = psum("score", [P, 2, 2 * QH])
        qk_max = psum("qk_max", [P, T])
        pv = psum("pv", [P, 2, QH])

        consts = sem("consts")
        qk_in = [sem(f"qk_in{i}") for i in range(GH)]
        v_in = [sem(f"v_in{i}") for i in range(GH)]
        maxrow_in = [sem(f"maxrow_in{i}") for i in range(GH)]
        max_ready = sem("max_ready")
        max_taken = sem("max_taken")
        parts_hi = sem("parts_hi")
        parts_done = sem("parts_done")
        turned = sem("turned")
        rows_done = sem("rows_done")
        score_ready = sem("score_ready")
        probs_ready = sem("probs_ready")
        vsq_ready = sem("vsq_ready")
        pv_done = sem("pv_done")
        pv_taken = sem("pv_taken")
        add_a_done = sem("add_a_done")
        add_b_done = sem("add_b_done")
        added0_done = sem("added0_done")
        added1_done = sem("added1_done")
        regrouped = [sem(f"regrouped{i}") for i in range(2)]
        sums_ready = sem("sums_ready")
        sums_taken = sem("sums_taken")
        sums_stored = sem("sums_stored")
        sums_in = sem("sums_in")
        recip_done = sem("recip_done")
        recipm_done = sem("recipm_done")
        recip_stored = sem("recip_stored")
        recip_in = sem("recip_in")
        folded = sem("folded")
        scaled = sem("scaled")
        meansq_done = sem("meansq_done")
        var_done = sem("var_done")
        relu_done = sem("relu_done")
        std_done = sem("std_done")
        x_in = sem("x_in")
        ab_done = sem("ab_done")
        xn_done = sem("xn_done")
        prod_done = sem("prod_done")
        out_done = sem("out_done")
        out_stored = sem("out_stored")

        block = ctx.enter_context(nc.Block())
        LAST = NG - 1

        def over_groups(eng, body):
            body(0)
            body(1)
            with eng.Fori(2, LAST) as g:
                body(g)
            body(LAST)

        def is_last(g):
            return isinstance(g, int) and g == LAST

        def is_first(g):
            return isinstance(g, int) and g == 0

        def has_head(g, j):
            return not (is_last(g) and j >= GH)

        @block.sync
        def _(sp):
            sp.dma_start(ident[:, :], ident_in).then_inc(consts, 16)

            def load_head(g, j):
                gg, s = g + j // GH, j % GH
                rows = bass.ds(gg * P + s * HD, HD)
                wait(sp, score_ready, MACROS * (4 * g + j - GH + 1))
                for part, (q_src, k_src) in enumerate(((q_hi, k_hi), (q_hi, k_lo), (q_lo, k_hi))):
                    at = slice(part * HD, (part + 1) * HD)
                    sp.dma_start(q_sb[at, s, :].bitcast(F32), q_src[rows, :]).then_inc(qk_in[s], 16)
                    sp.dma_start(k_sb[at, s, :].bitcast(F32), k_src[rows, :]).then_inc(qk_in[s], 16)
                sp.dma_start(k_sb[MASK_ROW:MASK_ROW + 1, s, :].bitcast(F32),
                             mask_b[bass.ds(gg, 1), :]).then_inc(qk_in[s], 16)
                wait(sp, vsq_ready, 2 * (4 * g + j - GH + 1))
                sp.dma_start(v_sb[:, s, :], v_t[bass.ds(gg * P, P), s * KT * HD:(s + 1) * KT * HD]
                             ).then_inc(v_in[s], 16)

            def load_maxrow(g, j):
                s = j % GH
                sp.wait_ge(rows_done, 4 * g + j + 1)
                for n in range(2):
                    sp.dma_start(q_sb[MAX_ROW + n:MAX_ROW + n + 1, s, :].bitcast(F32).rearrange(
                                     "a (t q) -> a t q", q=P),
                                 negmax_rows[n * KT:(n + 1) * KT, :].bitcast(F32)).then_inc(maxrow_in[s], 16)

            def regroup(g, j):
                jj = j % GH
                settled_wait(sp, pv_taken, 2 * (4 * g + j + 1))
                if jj == 0:
                    wait(sp, folded, 2 * (g + j // GH))
                for n, dst in enumerate((mean_a, sq_a, mean_b, sq_b)):
                    sp.dma_start(dst[jj * HD:(jj + 1) * HD, :], pv_sb[n * HD:(n + 1) * HD, j % 2, :]
                                 ).then_inc(regrouped[j % 2], 16)

            def sums_to_queries(f):
                sp.wait_ge(sums_taken, f + 1)
                sp.dma_start(sum_rows[bass.ds(f * GH, GH), :], sum_sb[0:P:HD, :]).then_inc(sums_stored, 16)
                sp.wait_ge(sums_stored, 16 * (f + 1))
                wait(sp, recipm_done, f)
                sp.dma_start(sum_c[:, :, :], sum_rows[bass.ds(f * GH, GH), :].rearrange(
                    "h (p e) -> p h e", p=P)).then_inc(sums_in, 16)
                sp.dma_start(mask_c[:, :], mask_f[bass.ds(f, 1), :].rearrange(
                    "a (p e) -> p (a e)", p=P)).then_inc(sums_in, 16)

            def recip_to_channels(f):
                sp.wait_ge(recipm_done, f + 1)
                sp.dma_start(recip_rows[bass.ds(f * GH, GH), :].rearrange("h (p e) -> p h e", p=P),
                             recip_m[:, :, :]).then_inc(recip_stored, 16)
                settled_wait(sp, recip_stored, 16 * (f + 1))
                wait(sp, scaled, 2 * f)
                for h in range(GH):
                    sp.dma_start(recip[h * HD:(h + 1) * HD, :],
                                 recip_rows[bass.ds(f * GH + h, 1), :].broadcast_to([HD, T])
                                 ).then_inc(recip_in, 16)

            def load_x(f):
                wait(sp, xn_done, f)
                wait(sp, out_done, f)
                sp.dma_start(x_sb[:, :], x_rows[bass.ds(f * P, P), :]).then_inc(x_in, 16)

            def store_out(f):
                sp.wait_ge(out_done, f + 1)
                sp.dma_start(out_rows[bass.ds(f * P, P), :], msq[:, :]).then_inc(out_stored, 16)

            sp.wait_ge(consts, 16 + 3)
            for j in range(3):
                load_head(0, j)
            load_maxrow(0, 0)

            def body(g):
                for j in range(GH):
                    if has_head(g, j + 1):
                        load_maxrow(g, j + 1)
                    if has_head(g, j + 3):
                        load_head(g, j + 3)
                    if not (is_first(g) and j == 0):
                        regroup(g if j else g - 1, j - 1 if j else GH - 1)
                    if not is_first(g):
                        if j == 0:
                            sums_to_queries(g - 1)
                        if j == 1:
                            recip_to_channels(g - 1)
                            load_x(g - 1)
                        if j == 3:
                            store_out(g - 1)

            over_groups(sp, body)
            regroup(LAST, GH - 1)
            sums_to_queries(LAST)
            recip_to_channels(LAST)
            load_x(LAST)
            store_out(LAST)
            sp.wait_ge(out_stored, 16 * NG)

        @block.tensor
        def _(pe):
            pe.wait_ge(consts, 16 + 3)

            def max_tile(g, j, n):
                s = j % GH
                if n == 0:
                    pe.wait_ge(qk_in[s], 7 * 16 * (g + j // GH + 1))
                wait(pe, max_taken, KT * (4 * g + j) + n)
                for half in range(2):
                    cols = slice(half * QH, (half + 1) * QH)
                    mm = pe.matmul(qk_max[:, cols], q_sb[0:MAX_ROW, s, n * P:(n + 1) * P],
                                   k_sb[0:MAX_ROW, s, cols], start=True, stop=True)
                mm.then_inc(max_ready, 1)

            def turn(g, j):
                pe.wait_ge(parts_done, 4 * g + j + 1)
                wait(pe, pv_taken, 2 * (4 * g + j - 1))
                pe.transpose(pv[0:2 * KT, 1, 0:P], negmax_parts[:, :], ident[:, :]).then_inc(turned, 1)

            def scores(g, j, m):
                if m == 0:
                    pe.wait_ge(maxrow_in[j], 32 * (g + 1))
                wait(pe, probs_ready, MACROS * (4 * g + j) + m - 1)
                for n in range(2):
                    kt = 2 * (m % 4) + n
                    mm = pe.matmul(score[:, m % 2, n * QH:(n + 1) * QH], k_sb[0:ROWS, j, kt * P:(kt + 1) * P],
                                   q_sb[0:ROWS, j, (m // 4) * QH:(m // 4 + 1) * QH], start=True, stop=True)
                mm.then_inc(score_ready, 1)

            def products(g, j, m):
                head, half = 4 * g + j, m // 4
                pe.wait_ge(probs_ready, MACROS * head + m + 1)
                if m == 0:
                    pe.wait_ge(vsq_ready, 2 * (head + 1))
                if m % 4 == 0:
                    wait(pe, pv_taken, 2 * head + half - 1)
                if m == 4 and has_head(g, j + 1):
                    pe.wait_ge(rows_done, head + 2)
                for n in range(2):
                    kt = 2 * (m % 4) + n
                    mm = pe.matmul(pv[64 * n:64 * n + 64, half, :], vv_sb[:, j, kt, :],
                                   probs[:, (2 * j + half) % 4, kt, :], start=(m % 4 == 0), stop=(m % 4 == 3))
                if m % 4 == 3:
                    mm.then_inc(pv_done, 1)

            def sums(f):
                pe.wait_ge(added0_done, 4 * f + 4)
                pe.wait_ge(added1_done, 4 * f + 4)
                for half in range(2):
                    for part in range(2):
                        for h in range(GH):
                            mm = pe.matmul(qk_max[h * HD:(h + 1) * HD, half * QH:(half + 1) * QH], ones[:, :],
                                           added[:, half, h, part, :], start=(part == 0), stop=(part == 1))
                mm.then_inc(sums_ready, 1)

            for n in range(KT):
                max_tile(0, 0, n)
            turn(0, 0)
            for n in range(KT):
                max_tile(0, 1, n)

            def body(g):
                for j in range(GH):
                    for m in range(MACROS):
                        scores(g, j, m)
                        if m:
                            products(g, j, m - 1)
                        elif j:
                            products(g, j - 1, MACROS - 1)
                        elif not is_first(g):
                            products(g - 1, GH - 1, MACROS - 1)
                        if m == 2 and has_head(g, j + 1):
                            turn(g, j + 1)
                        if j == 0 and m == 5 and not is_first(g):
                            pe.wait_ge(max_taken, KT * (4 * g + 2) + m)
                            sums(g - 1)
                        if j == 0 and m == 5 and not is_first(g):
                            pe.wait_ge(sums_taken, g)
                        if has_head(g, j + 2):
                            max_tile(g, j + 2, m)

            over_groups(pe, body)
            products(LAST, GH - 1, MACROS - 1)
            sums(LAST)

        @block.scalar
        def _(act):
            def square_v(g, j):
                s = j % GH
                act.wait_ge(v_in[s], 16 * (g + j // GH + 1))
                wait(act, pv_done, 2 * (4 * g + j - GH + 1))
                v = v_sb[:, s, :].rearrange("p (k d) -> p k d", d=HD)
                act.activation(vv_sb[:, s, :, 0:HD], v, ACT.Copy).then_inc(vsq_ready, 1)
                act.activation(vv_sb[:, s, :, HD:2 * HD], v, ACT.Square).then_inc(vsq_ready, 1)

            def exp(g, j, m):
                head, half = 4 * g + j, m // 4
                unit = 2 * head + half
                act.wait_ge(score_ready, MACROS * head + m + 1)
                if m % 4 == 0:
                    wait(act, pv_done, unit - 3)
                    wait(act, add_a_done, unit - 3)
                    wait(act, add_b_done, unit - 3)
                kt = 2 * (m % 4)
                act.activation(probs[:, (2 * j + half) % 4, kt:kt + 2, :].rearrange("p k q -> p (k q)"),
                               score[:, m % 2, :], ACT.Exp, scale=SCALE).then_inc(probs_ready, 1)

            def take_pv(g, j, half):
                head = 4 * g + j
                act.wait_ge(pv_done, 2 * head + half + 1)
                if half == 0:
                    wait(act, regrouped[j % 2], 64 * (2 * g + j // 2))
                act.activation(pv_sb[:, j % 2, half * QH:(half + 1) * QH], pv[:, half, :],
                               ACT.Copy).then_inc(pv_taken, 1)

            def take_sums(f):
                act.wait_ge(sums_ready, f + 1)
                wait(act, sums_stored, 16 * f)
                act.activation(sum_sb[:, :], qk_max[:, :], ACT.Copy).then_inc(sums_taken, 1)

            def mean_squared(f):
                act.wait_ge(scaled, 2 * f + 2)
                wait(act, prod_done, f)
                act.activation(std[:, :], mean[:, :], ACT.Square).then_inc(meansq_done, 1)

            def normalise(f):
                act.wait_ge(x_in, 16 * (f + 1))
                act.wait_ge(ab_done, 2 * (f + 1))
                act.activation(x_sb[:, :], x_sb[:, :], ACT.Identity, bias=ab[:, 1:2],
                               scale=ab[:, 0:1]).then_inc(xn_done, 1)

            def root(f):
                act.wait_ge(var_done, f + 1)
                act.activation(std[:, :], msq[:, :], ACT.Relu).then_inc(relu_done, 1)
                act.wait_ge(relu_done, f + 1)
                act.activation(std[:, :], std[:, :], ACT.Sqrt).then_inc(std_done, 1)

            square_v(0, 0)

            def body(g):
                for j in range(GH):
                    for m in range(MACROS):
                        exp(g, j, m)
                        if m == 1 and j:
                            take_pv(g, j - 1, 1)
                        if m == 1 and not j and not is_first(g):
                            take_pv(g - 1, GH - 1, 1)
                        if m == 5:
                            take_pv(g, j, 0)
                        if m == 5 and j == 0 and not is_first(g):
                            take_sums(g - 1)
                        if m == 6 and has_head(g, j + 1):
                            square_v(g, j + 1)
                        if not is_first(g):
                            if j == 2 and m == 2:
                                mean_squared(g - 1)
                            if j == 2 and m == 3:
                                normalise(g - 1)
                            if j == 3 and m == 0:
                                root(g - 1)

            over_groups(act, body)
            take_pv(LAST, GH - 1, 1)
            take_sums(LAST)
            mean_squared(LAST)
            normalise(LAST)
            root(LAST)

        @block.vector
        def _(dve):
            dve.memset(q_sb[MASK_ROW:ROWS, :, :].bitcast(F32), 1.0).then_inc(consts, 1)
            dve.memset(k_sb[MASK_ROW:ROWS, :, :].bitcast(F32), 1.0).then_inc(consts, 1)
            dve.memset(ones[:, :], 1.0).then_inc(consts, 1)

            def take_max(g, j, n):
                head = 4 * g + j
                dve.wait_ge(max_ready, KT * head + n + 1)
                if n == 0:
                    wait(dve, parts_done, head)
                dve.tensor_reduce(negmax[:, n:n + 1], qk_max[:, :], AX_X, ALU.max,
                                  negate=True).then_inc(max_taken, 1)

            def split_max(g, j):
                head = 4 * g + j
                settled_wait(dve, max_taken, KT * (head + 1))
                wait(dve, turned, head)
                dve.tensor_copy(negmax_parts[:, 0:KT].bitcast(F32R), negmax[:, :]).then_inc(parts_hi, 1)
                dve.wait_ge(parts_hi, head + 1)
                dve.tensor_tensor(negmax_parts[:, KT:2 * KT].bitcast(F32R), negmax[:, :], negmax_parts[:, 0:KT],
                                  ALU.subtract).then_inc(parts_done, 1)

            def take_rows(g, j):
                head = 4 * g + j
                dve.wait_ge(turned, head + 1)
                if j:
                    dve.wait_ge(maxrow_in[j - 1], 32 * (g + 1))
                dve.tensor_copy(negmax_rows[:, :], pv[0:2 * KT, 1, 0:P]).then_inc(rows_done, 1)

            def add_first(g, j, half):
                head = 4 * g + j
                unit = 2 * head + half
                u = (2 * j + half) % 4
                dve.wait_ge(probs_ready, 4 * unit + 2)
                if half == 0:
                    wait(dve, added0_done, head)
                else:
                    wait(dve, added1_done, head)
                flat = probs[:, u, :, :].rearrange("p k q -> p (k q)")
                dve.tensor_tensor(add_a[:, half, :], flat[:, 0:2 * QH], flat[:, 2 * QH:4 * QH],
                                  ALU.add).then_inc(add_a_done, 1)

            def add_all(g, j):
                head = 4 * g + j
                dve.wait_ge(add_b_done, 2 * head + 1)
                dve.wait_ge(add_a_done, 2 * head + 1)
                if j == 0:
                    wait(dve, sums_ready, g)
                dve.tensor_tensor(added[:, 0, j, :, :].rearrange("p k q -> p (k q)"), add_a[:, 0, :],
                                  add_b[:, 0, :], ALU.add).then_inc(added0_done, 1)

            def invert(f):
                settled_wait(dve, sums_in, 32 * (f + 1))
                wait(dve, recipm_done, f)
                dve.reciprocal(recip_c[:, :, :], sum_c[:, :, :]).then_inc(recip_done, 1)
                settled_wait(dve, recip_done, f + 1)
                wait(dve, recip_stored, 16 * f)
                dve.tensor_tensor(recip_m[:, :, :], recip_c[:, :, :],
                                  mask_c[:, :].rearrange("p (a e) -> p a e", a=1).broadcast_to([P, GH, T // P]),
                                  ALU.mult).then_inc(recipm_done, 1)

            def take_ab(f):
                wait(dve, xn_done, f)
                for n in range(2):
                    dve.tensor_copy(ab[:, n:n + 1], norm_ab[:, n, bass.ds(f, 1)]).then_inc(ab_done, 1)

            def variance(f):
                dve.wait_ge(meansq_done, f + 1)
                dve.tensor_tensor(msq[:, :], msq[:, :], std[:, :], ALU.subtract).then_inc(var_done, 1)

            def times_std(f):
                dve.wait_ge(std_done, f + 1)
                dve.wait_ge(xn_done, f + 1)
                dve.tensor_tensor(x_sb[:, :], x_sb[:, :], std[:, :], ALU.mult).then_inc(prod_done, 1)

            def plus_mean(f):
                dve.wait_ge(prod_done, f + 1)
                dve.tensor_tensor(msq[:, :], x_sb[:, :], mean[:, :], ALU.add).then_inc(out_done, 1)

            for n in range(KT):
                take_max(0, 0, n)
            split_max(0, 0)
            take_rows(0, 0)
            for n in range(KT):
                take_max(0, 1, n)

            def body(g):
                for j in range(GH):
                    if has_head(g, j + 1):
                        split_max(g, j + 1)
                    for m in range(MACROS):
                        if has_head(g, j + 2):
                            take_max(g, j + 2, m)
                        if m == 1 and has_head(g, j + 1):
                            take_rows(g, j + 1)
                        if m == 2:
                            add_first(g, j, 0)
                        if m == 4:
                            add_all(g, j)
                        if m == 5:
                            add_first(g, j, 1)
                        if not is_first(g):
                            if j == 1 and m == 0:
                                invert(g - 1)
                                take_ab(g - 1)
                            if j == 2 and m == 4:
                                variance(g - 1)
                            if j == 3 and m == 3:
                                times_std(g - 1)
                            if j == 3 and m == 6:
                                plus_mean(g - 1)

            over_groups(dve, body)
            invert(LAST)
            take_ab(LAST)
            variance(LAST)
            times_std(LAST)
            plus_mean(LAST)

        @block.gpsimd
        def _(pool):
            def add_last(g, j, half):
                head = 4 * g + j
                unit = 2 * head + half
                u = (2 * j + half) % 4
                pool.wait_ge(probs_ready, 4 * unit + 4)
                if half == 0:
                    wait(pool, added0_done, head)
                else:
                    wait(pool, added1_done, head)
                flat = probs[:, u, :, :].rearrange("p k q -> p (k q)")
                pool.tensor_tensor(add_b[:, half, :], flat[:, 4 * QH:6 * QH], flat[:, 6 * QH:8 * QH],
                                   ALU.add).then_inc(add_b_done, 1)

            def add_all(g, j):
                head = 4 * g + j
                pool.wait_ge(add_a_done, 2 * head + 2)
                pool.wait_ge(add_b_done, 2 * head + 2)
                if j == 0:
                    wait(pool, sums_ready, g)
                pool.tensor_tensor(added[:, 1, j, :, :].rearrange("p k q -> p (k q)"), add_a[:, 1, :],
                                   add_b[:, 1, :], ALU.add).then_inc(added1_done, 1)

            def fold(f):
                for s in regrouped:
                    pool.wait_ge(s, 128 * (f + 1))
                wait(pool, out_done, f)
                wait(pool, out_stored, 16 * f)
                pool.tensor_tensor(mean[:, :], mean_a[:, :], mean_b[:, :], ALU.add).then_inc(folded, 1)
                pool.tensor_tensor(msq[:, :], sq_a[:, :], sq_b[:, :], ALU.add).then_inc(folded, 1)

            def divide(f):
                pool.wait_ge(recip_in, 64 * (f + 1))
                pool.wait_ge(folded, 2 * (f + 1))
                pool.tensor_tensor(mean[:, :], mean[:, :], recip[:, :], ALU.mult).then_inc(scaled, 1)
                pool.tensor_tensor(msq[:, :], msq[:, :], recip[:, :], ALU.mult).then_inc(scaled, 1)

            def body(g):
                for j in range(GH):
                    if j:
                        add_last(g, j - 1, 1)
                        add_all(g, j - 1)
                    elif not is_first(g):
                        add_last(g - 1, GH - 1, 1)
                        add_all(g - 1, GH - 1)
                    add_last(g, j, 0)
                    if not is_first(g):
                        if j == 0:
                            fold(g - 1)
                        if j == 1:
                            divide(g - 1)

            over_groups(pool, body)
            add_last(LAST, GH - 1, 1)
            add_all(LAST, GH - 1)
            fold(LAST)
            divide(LAST)


def cross_attention(nc, x, kv, mask, wqT, bq, wkT, bk, wvT, bv, ident_in, out):
    B, C, T = x.shape
    groups = B * C // P

    def dram(name, shape):
        return nc.dram_tensor(name, shape, F32, kind="Internal").ap()

    scratch = [dram(n, (B * C, T)) for n in ("q_hi", "q_lo", "k_hi", "k_lo", "v_rows")]
    scratch += [dram(n, (groups, T)) for n in ("mask_rows", "mask_bias_rows")]
    sum_rows = dram("sum_rows", (groups * 4, T))
    recip_rows = dram("recip_rows", (groups * 4, T))
    with nc.sbuf_tensor("norm_ab", [P, 2, groups], F32) as norm_ab:
        project(nc, x, kv, mask, wqT, bq, wkT, bk, wvT, bv, scratch, norm_ab)
        attend(nc, x, out, ident_in, scratch, sum_rows, recip_rows, norm_ab)


def kernel(x, ctx_2048, mask_Bx1x2048_bf1, L0_xattn_Wq, L0_xattn_bq, L0_xattn_Wk, L0_xattn_bk, L0_xattn_Wv,
           L0_xattn_bv):
    import numpy as np
    import concourse.bacc as bacc
    from concourse.bass_utils import run_bass_kernel_spmd

    arrays = {
        "x": np.ascontiguousarray(x),
        "kv": np.ascontiguousarray(ctx_2048),
        "mask": np.ascontiguousarray(mask_Bx1x2048_bf1),
        "wq_t": np.ascontiguousarray(np.asarray(L0_xattn_Wq).T),
        "bq": np.ascontiguousarray(np.asarray(L0_xattn_bq).reshape(-1, P).T),
        "wk_t": np.ascontiguousarray(np.asarray(L0_xattn_Wk).T),
        "bk": np.ascontiguousarray(np.asarray(L0_xattn_bk).reshape(-1, P).T),
        "wv_t": np.ascontiguousarray(np.asarray(L0_xattn_Wv).T),
        "bv": np.ascontiguousarray(L0_xattn_bv),
        "identity": np.eye(P, dtype=np.float32),
    }
    nc = bacc.Bacc("TRN2", target_bir_lowering=False, num_devices=1)
    args = [nc.dram_tensor(n, a.shape, mybir.dt.from_np(a.dtype), kind="ExternalInput").ap()
            for n, a in arrays.items()]
    out = nc.dram_tensor("out", arrays["x"].shape, F32, kind="ExternalOutput").ap()
    cross_attention(nc, *args, out)
    return run_bass_kernel_spmd(nc, [arrays], core_ids=[0]).results[0]["out"]
```

```python
from contextlib import ExitStack

import concourse.bass as bass
from concourse import mybir

F32 = mybir.dt.float32
F32R = mybir.dt.float32r
U8 = mybir.dt.uint8
ALU = mybir.AluOpType
ACT = mybir.ActivationFunctionType
AX_X = mybir.AxisListType.X

P = 128
EPS = 1e-5
MASKED = 2.0 ** 127


def wait(eng, sem, value):
    if isinstance(value, int) and value <= 0:
        return
    eng.wait_ge(sem, value)


def settled_wait(eng, sem, value):
    wait(eng, sem, value)
    if not isinstance(value, int):
        eng.nop(nofuse=True)


def project(nc, x, kv, mask, wqT, bq, wkT, bk, wvT, bv, scratch, norm_ab):
    B, C, T = x.shape
    CT = C // P
    TT = T // P
    HALF = 512
    NH = T // HALF
    HD = 32
    HEADS = C // HD
    BANKS = 8
    TILES = CT * NH
    TPB = 2 * TILES + TT
    assert TPB % BANKS == 0 and CT == 4 and NH == 2
    q_hi, q_lo, k_hi, k_lo, v_t, mask_f, mask_b = scratch

    with ExitStack() as ctx:
        def sb(name, shape, dt):
            return ctx.enter_context(nc.sbuf_tensor(name, shape, dt))

        def sem(name):
            return ctx.enter_context(nc.semaphore(name))

        w_hi = sb("w_hi", [P, 3, CT, C], F32R)
        w_lo = sb("w_lo", [P, 3, CT, C], F32R)
        raw = sb("raw", [P, 4, T], F32)
        in_hi = sb("in_hi", [P, 2 * CT, T], F32R)
        in_lo = sb("in_lo", [P, 2 * CT, T], F32R)
        out_hi = sb("out_hi", [P, 2, T], F32R)
        out_lo = sb("out_lo", [P, 2, T], F32R)
        v_sb = sb("v_sb", [P, HEADS, TT, HD], F32)
        xm = sb("xm", [P, T], F32)
        junk = sb("junk", [P, T], F32)
        mask_u8 = sb("mask_u8", [P, T], U8)
        mask_sb = sb("mask_sb", [P, T], F32)
        mask_row = sb("mask_row", [1, T], F32)
        bqk = sb("bqk", [P, 2, CT], F32)
        bv_sb = sb("bv_sb", [P, C], F32)
        sum4 = sb("sum4", [P, CT], F32)
        sq4 = sb("sq4", [P, CT], F32)
        sums = sb("sums", [P, B * CT], F32)
        sqs = sb("sqs", [P, B * CT], F32)
        nval = sb("nval", [P, B], F32)
        rn = sb("rn", [P, B], F32)
        mean = sb("mean", [P, B * CT], F32)
        mean2 = sb("mean2", [P, B * CT], F32)
        var = sb("var", [P, B * CT], F32)
        ps = [ctx.enter_context(nc.psum_tensor(f"proj{i}", [P, HALF], F32)) for i in range(BANKS)]

        w_in = [sem(f"w_in{i}") for i in range(3)]
        w_hi_done = sem("w_hi_done")
        w_lo_done = sem("w_lo_done")
        consts_in = sem("consts_in")
        raw_in = [sem(f"raw_in{i}") for i in range(4)]
        mask_in = sem("mask_in")
        hi_done = sem("hi_done")
        lo_done = sem("lo_done")
        mask_done = sem("mask_done")
        maskrow_done = sem("maskrow_done")
        nval_done = sem("nval_done")
        xm_done = sem("xm_done")
        sq_done = sem("sq_done")
        stat_done = sem("stat_done")
        mm_done = sem("mm_done")
        outhi_done = sem("outhi_done")
        evac_done = sem("evac_done")
        stored = [sem(f"stored{i}") for i in range(2)]
        v_stored = sem("v_stored")
        mask_stored = sem("mask_stored")
        chain = sem("chain")
        root = sem("root")

        block = ctx.enter_context(nc.Block())

        def over_batches(eng, body):
            body(0)
            with eng.Fori(1, B - 1) as b:
                body(b)
            body(B - 1, last=True)

        @block.sync
        def _(sp):
            def load_w(j, w):
                if j == 2:
                    sp.wait_ge(w_lo_done, 1)
                half = raw[:, 2 * (j % 2):2 * (j % 2) + 2, :].rearrange("p s (c o) -> p (s c) o", o=C)
                sp.dma_start(half, w.rearrange("(c p) o -> p c o", p=P)).then_inc(w_in[j], 16)

            load_w(0, wqT)
            load_w(1, wkT)
            load_w(2, wvT)
            sp.dma_start(bqk[:, 0, :], bq).then_inc(consts_in, 16)
            sp.dma_start(bqk[:, 1, :], bk).then_inc(consts_in, 16)
            sp.dma_start(bv_sb[:, :], bv.rearrange("(a o) -> a o", a=1).broadcast_to([P, C])).then_inc(consts_in, 16)

            def load_inputs(b, src, first):
                for r in range(CT):
                    if first == 0:
                        if isinstance(b, int) and b == 0:
                            sp.wait_ge(w_lo_done, 3 if r < 2 else 2)
                        else:
                            sp.wait_ge(lo_done, 8 * b - 3 + r)
                    else:
                        settled_wait(sp, lo_done, 8 * b + 1 + r)
                        sp.wait_ge(xm_done, 4 * b + 1 + r)
                    sp.dma_start(raw[:, r, :], src[b, r * P:(r + 1) * P, :] if isinstance(b, int)
                                 else src[bass.ds(b, 1), r * P:(r + 1) * P, :].rearrange("a p t -> (a p) t")
                                 ).then_inc(raw_in[r], 16)

            def load_mask(b):
                settled_wait(sp, mask_done, b)
                row = mask[b] if isinstance(b, int) else mask[bass.ds(b, 1)].rearrange("a o t -> (a o) t")
                sp.dma_start(mask_u8[:, :], row.broadcast_to([P, T])).then_inc(mask_in, 16)

            def store_masks(b):
                sp.wait_ge(maskrow_done, b + 1)
                for g in range(CT):
                    sp.dma_start(mask_f[bass.ds(b * CT + g, 1), :], mask_sb[0:1, :]).then_inc(mask_stored, 16)
                    sp.dma_start(mask_b[bass.ds(b * CT + g, 1), :], mask_row[:, :]).then_inc(mask_stored, 16)

            load_mask(0)
            load_inputs(0, x, 0)
            store_masks(0)
            load_inputs(0, kv, 4)

            def body(b, last=False):
                if not last:
                    load_mask(b + 1)
                    load_inputs(b + 1, x, 0)

                def store(n, hi, lo):
                    for o in range(CT):
                        sp.wait_ge(evac_done, TPB * b + 2 * (n + o) + 2)
                        rows = bass.ds(b * C + o * P, P)
                        sp.dma_start(hi[rows, :], out_hi[:, o % 2, :].bitcast(F32)).then_inc(stored[o % 2], 16)
                        sp.dma_start(lo[rows, :], out_lo[:, o % 2, :].bitcast(F32)).then_inc(stored[o % 2], 16)

                store(0, q_hi, q_lo)
                if not last:
                    store_masks(b + 1)
                    load_inputs(b + 1, kv, 4)
                store(4, k_hi, k_lo)
                sp.wait_ge(evac_done, TPB * b + TPB)
                for g in range(CT):
                    sp.dma_start(v_t[bass.ds(b * C + g * P, P), :],
                                 v_sb[:, 4 * g:4 * g + 4, :, :].rearrange("p h t d -> p (h t d)")
                                 ).then_inc(v_stored, 16)

            over_batches(sp, body)
            for s in stored:
                sp.wait_ge(s, B * 4 * 32)
            sp.wait_ge(v_stored, B * CT * 16)
            sp.wait_ge(mask_stored, B * CT * 32)

        @block.scalar
        def _(act):
            for j in range(3):
                act.wait_ge(w_in[j], 16)
                half = raw[:, 2 * (j % 2):2 * (j % 2) + 2, :].rearrange("p s (c o) -> p (s c) o", o=C)
                act.activation(w_hi[:, j, :, :], half, ACT.Copy).then_inc(w_hi_done, 1)

            def split(b, first):
                for r in range(CT):
                    wait(act, mm_done, TPB * b - TPB + TILES if first == 0 else TPB * b)
                    act.wait_ge(raw_in[r], 32 * b + (16 if first == 0 else 32))
                    act.activation(in_hi[:, first + r, :], raw[:, r, :], ACT.Copy).then_inc(hi_done, 1)
                    if first == 0:
                        act.wait_ge(xm_done, 4 * b + r + 1)
                        wait(act, sq_done, 4 * b + r)
                        if r == 0:
                            wait(act, stat_done, 2 * b)
                        act.activation(junk[:, :], xm[:, :], ACT.Square,
                                       accum_out=sq4[:, r:r + 1]).then_inc(sq_done, 1)

            def evacuate_hi(b, n):
                for i in range(TILES):
                    o, half = i // NH, i % NH
                    t = TILES * n + i
                    act.wait_ge(mm_done, TPB * b + t + 1)
                    if half == 0:
                        wait(act, stored[o % 2], 32 * (4 * b + 2 * n + o // 2))
                    act.activation(out_hi[:, o % 2, half * HALF:(half + 1) * HALF], ps[t % BANKS][:, :],
                                   ACT.Identity, bias=bqk[:, n, o:o + 1]).then_inc(outhi_done, 1)

            act.wait_ge(consts_in, 48)
            split(0, 0)
            split(0, 4)

            def body(b, last=False):
                evacuate_hi(b, 0)
                if not last:
                    split(b + 1, 0)
                evacuate_hi(b, 1)
                if not last:
                    split(b + 1, 4)

            over_batches(act, body)
            act.wait_ge(chain, 5)
            act.activation(mean2[:, :], var[:, :], ACT.Sqrt).then_inc(root, 1)

        @block.vector
        def _(dve):
            for j in range(3):
                dve.wait_ge(w_hi_done, j + 1)
                half = raw[:, 2 * (j % 2):2 * (j % 2) + 2, :].rearrange("p s (c o) -> p (s c) o", o=C)
                dve.tensor_tensor(w_lo[:, j, :, :], half, w_hi[:, j, :, :].bitcast(F32),
                                  ALU.subtract).then_inc(w_lo_done, 1)

            def take_mask(b):
                settled_wait(dve, mask_in, 16 * b + 16)
                settled_wait(dve, mask_stored, 32 * CT * b)
                wait(dve, xm_done, 4 * b)
                dve.tensor_copy(mask_sb[:, :], mask_u8[:, :]).then_inc(mask_done, 1)
                dve.wait_ge(mask_done, b + 1)
                dve.tensor_scalar(mask_row[:, :], mask_sb[0:1, :], MASKED, -MASKED, ALU.mult,
                                  ALU.add).then_inc(maskrow_done, 1)
                dve.tensor_reduce(nval[:, bass.ds(b, 1)], mask_sb[:, :], AX_X, ALU.add).then_inc(nval_done, 1)

            def split(b, first):
                if first == 0:
                    take_mask(b)
                for r in range(CT):
                    dve.wait_ge(hi_done, 8 * b + first + r + 1)
                    wait(dve, mm_done, TPB * b - TPB + TILES if first == 0 else TPB * b)
                    dve.tensor_tensor(in_lo[:, first + r, :], raw[:, r, :], in_hi[:, first + r, :].bitcast(F32),
                                      ALU.subtract).then_inc(lo_done, 1)
                    if first == 0:
                        settled_wait(dve, sq_done, 4 * b + r)
                        if r == 0:
                            wait(dve, stat_done, 2 * b)
                        wait(dve, xm_done, 4 * b + r)
                        dve.tensor_tensor_reduce(xm[:, :], raw[:, r, :], mask_sb[:, :], 1.0, 0.0, ALU.mult,
                                                 ALU.add, sum4[:, r:r + 1]).then_inc(xm_done, 1)
                if first == 0:
                    dve.wait_ge(xm_done, 4 * b + 4)
                    dve.tensor_copy(sums[:, bass.ds(b * CT, CT)], sum4[:, :]).then_inc(stat_done, 1)
                    settled_wait(dve, sq_done, 4 * b + 4)
                    dve.tensor_copy(sqs[:, bass.ds(b * CT, CT)], sq4[:, :]).then_inc(stat_done, 1)

            def evacuate_lo(b, n):
                for i in range(TILES):
                    o, half = i // NH, i % NH
                    t = TILES * n + i
                    dve.wait_ge(outhi_done, 2 * TILES * b + t + 1)
                    if half == 0:
                        wait(dve, stored[o % 2], 32 * (4 * b + 2 * n + o // 2))
                    cols = slice(half * HALF, (half + 1) * HALF)
                    dve.scalar_tensor_tensor(out_lo[:, o % 2, cols], ps[t % BANKS][:, :], bqk[:, n, o:o + 1],
                                             out_hi[:, o % 2, cols].bitcast(F32), ALU.add,
                                             ALU.subtract).then_inc(evac_done, 1)

            def evacuate_v(b):
                for i in range(TT):
                    t = 2 * TILES + i
                    settled_wait(dve, mm_done, TPB * b + t + 1)
                    wait(dve, v_stored, 16 * CT * b)
                    dve.tensor_tensor(v_sb[:, :, i, :], ps[t % BANKS][:, :].rearrange("p (h d) -> p h d", d=HD),
                                      bv_sb[:, :].rearrange("p (h d) -> p h d", d=HD),
                                      ALU.add).then_inc(evac_done, 1)

            dve.wait_ge(consts_in, 48)
            split(0, 0)
            split(0, 4)

            def body(b, last=False):
                evacuate_lo(b, 0)
                if not last:
                    split(b + 1, 0)
                evacuate_lo(b, 1)
                evacuate_v(b)
                if not last:
                    split(b + 1, 4)

            over_batches(dve, body)

            dve.wait_ge(stat_done, 2 * B)
            dve.wait_ge(nval_done, B)
            dve.reciprocal(rn[:, :], nval[:, :]).then_inc(chain, 1)
            dve.wait_ge(chain, 1)
            by_batch = rn[:, :].rearrange("p (b o) -> p b o", o=1).broadcast_to([P, B, CT])

            def grouped(t):
                return t[:, :].rearrange("p (b c) -> p b c", c=CT)

            dve.tensor_tensor(grouped(mean), grouped(sums), by_batch, ALU.mult).then_inc(chain, 1)
            dve.tensor_tensor(grouped(var), grouped(sqs), by_batch, ALU.mult).then_inc(chain, 1)
            dve.wait_ge(chain, 3)
            dve.tensor_tensor(mean2[:, :], mean[:, :], mean[:, :], ALU.mult).then_inc(chain, 1)
            dve.wait_ge(chain, 4)
            dve.tensor_tensor(sqs[:, :], var[:, :], mean2[:, :], ALU.subtract).then_inc(root, 1)
            dve.wait_ge(root, 1)
            dve.tensor_scalar(var[:, :], sqs[:, :], 0.0, EPS, ALU.max, ALU.add).then_inc(chain, 1)
            dve.wait_ge(root, 2)
            dve.reciprocal(norm_ab[:, 0, :], mean2[:, :]).then_inc(chain, 1)
            dve.wait_ge(chain, 6)
            dve.scalar_tensor_tensor(norm_ab[:, 1, :], mean[:, :], -1.0, norm_ab[:, 0, :], ALU.mult,
                                     ALU.mult).then_inc(chain, 1)
            dve.wait_ge(chain, 7)

        @block.tensor
        def _(pe):
            pe.wait_ge(w_lo_done, 3)

            def products(b, t, pairs):
                wait(pe, evac_done, TPB * b + t - BANKS + 1)
                for n, (lhsT, rhs) in enumerate(pairs):
                    mm = pe.matmul(ps[t % BANKS][:, :], lhsT, rhs, start=(n == 0), stop=(n == len(pairs) - 1))
                mm.then_inc(mm_done, 1)

            def parts(a_hi, a_lo, b_hi, b_lo):
                return [(a_hi, b_hi), (a_hi, b_lo), (a_lo, b_hi)]

            def body(b, last=False):
                for n in range(2):
                    pe.wait_ge(lo_done, 8 * b + 4 + 4 * n)
                    for i in range(TILES):
                        out = slice((i // NH) * P, (i // NH + 1) * P)
                        cols = slice((i % NH) * HALF, (i % NH + 1) * HALF)
                        pairs = []
                        for c in range(CT):
                            pairs += parts(w_hi[:, n, c, out], w_lo[:, n, c, out],
                                           in_hi[:, 4 * n + c, cols], in_lo[:, 4 * n + c, cols])
                        products(b, TILES * n + i, pairs)
                for i in range(TT):
                    rows = slice(i * P, (i + 1) * P)
                    pairs = []
                    for c in range(CT):
                        pairs += parts(in_hi[:, 4 + c, rows], in_lo[:, 4 + c, rows],
                                       w_hi[:, 2, c, :], w_lo[:, 2, c, :])
                    products(b, 2 * TILES + i, pairs)

            over_batches(pe, body)


def attend(nc, x, out, ident_in, scratch, sum_rows, recip_rows, norm_ab):
    B, C, T = x.shape
    HD = 32
    GH = P // HD
    NG = B * C // P
    KT = T // P
    QH = 512
    SCALE = float(HD) ** -0.5
    MASK_ROW, MAX_ROW, ROWS = 3 * HD, 3 * HD + 1, 3 * HD + 3
    MACROS = 8
    assert GH == 4 and KT == 8 and T == 2 * QH
    q_hi, q_lo, k_hi, k_lo, v_t, mask_f, mask_b = scratch
    x_rows = x.rearrange("b c t -> (b c) t")
    out_rows = out.rearrange("b c t -> (b c) t")

    with ExitStack() as ctx:
        def sb(name, shape, dt):
            return ctx.enter_context(nc.sbuf_tensor(name, shape, dt))

        def psum(name, shape):
            return ctx.enter_context(nc.psum_tensor(name, shape, F32))

        def sem(name):
            return ctx.enter_context(nc.semaphore(name))

        q_sb = sb("q_sb", [P, GH, T], F32R)
        k_sb = sb("k_sb", [P, GH, T], F32R)
        v_sb = sb("v_sb_", [P, GH, KT * HD], F32)
        vv_sb = sb("vv_sb", [P, GH, KT, 2 * HD], F32)
        probs = sb("probs", [P, 4, KT, QH], F32)
        added = sb("added", [P, 2, GH, 2, QH], F32)
        pv_sb = sb("pv_sb", [P, 2, T], F32)
        mean_a = sb("mean_a", [P, T], F32)
        mean_b = sb("mean_b", [P, T], F32)
        sq_a = sb("sq_a", [P, T], F32)
        sq_b = sb("sq_b", [P, T], F32)
        mean_raw = sb("mean_raw", [P, T], F32)
        sq_raw = sb("sq_raw", [P, T], F32)
        mean = sb("mean_", [P, T], F32)
        sq = sb("sq", [P, T], F32)
        std = sb("std", [P, T], F32)
        x_sb = sb("x_sb", [P, T], F32)
        recip = sb("recip", [P, T], F32)
        sum_sb = sb("sum_sb", [P, T], F32)
        sum_c = sb("sum_c", [P, GH, T // P], F32)
        recip_c = sb("recip_c", [P, GH, T // P], F32)
        recip_m = sb("recip_m", [P, GH, T // P], F32)
        mask_c = sb("mask_c", [P, T // P], F32)
        negmax2 = sb("negmax2", [P, 2, 2, KT], F32)
        negmax = sb("negmax", [P, KT], F32)
        negmax_parts = sb("negmax_parts", [P, 2 * KT], F32)
        negmax_rows = sb("negmax_rows", [2 * KT, P], F32R)
        ab = sb("ab", [P, 2], F32)
        ones = sb("ones", [P, HD], F32)
        ident = sb("ident", [P, P], F32)

        score = psum("score", [P, 2, 2 * QH])
        qk_max = psum("qk_max", [P, T])
        pv = psum("pv", [P, 2, QH])

        consts = sem("consts")
        qk_in = [sem(f"qk_in{i}") for i in range(GH)]
        v_in = [sem(f"v_in{i}") for i in range(GH)]
        maxrow_in = [sem(f"maxrow_in{i}") for i in range(GH)]
        max_ready = sem("max_ready")
        max_taken = sem("max_taken")
        negmax_done = sem("negmax_done")
        parts_hi = sem("parts_hi")
        parts_done = sem("parts_done")
        turned = sem("turned")
        rows_done = sem("rows_done")
        score_ready = sem("score_ready")
        probs_ready = sem("probs_ready")
        vsq_ready = sem("vsq_ready")
        pv_done = sem("pv_done")
        pv_taken = sem("pv_taken")
        first_added = sem("first_added")
        last_added = sem("last_added")
        all_added = sem("all_added")
        totalled = sem("totalled")
        regrouped = [sem(f"regrouped{i}") for i in range(2)]
        sums_ready = sem("sums_ready")
        sums_taken = sem("sums_taken")
        sums_stored = sem("sums_stored")
        sums_in = sem("sums_in")
        recip_done = sem("recip_done")
        recipm_done = sem("recipm_done")
        recip_stored = sem("recip_stored")
        recip_in = sem("recip_in")
        folded = sem("folded")
        scaled = sem("scaled")
        meansq_done = sem("meansq_done")
        var_done = sem("var_done")
        relu_done = sem("relu_done")
        std_done = sem("std_done")
        x_in = sem("x_in")
        ab_done = sem("ab_done")
        xn_done = sem("xn_done")
        prod_done = sem("prod_done")
        out_done = sem("out_done")
        out_stored = sem("out_stored")

        block = ctx.enter_context(nc.Block())
        LAST = NG - 1

        def over_groups(eng, body):
            for g in range(3):
                body(g)
            with eng.Fori(3, LAST) as g:
                body(g)
            body(LAST)

        def is_last(g):
            return isinstance(g, int) and g == LAST

        def exists(f):
            return not isinstance(f, int) or f >= 0

        def has_head(g, j):
            return not (is_last(g) and j >= GH)

        @block.sync
        def _(sp):
            sp.dma_start(ident[:, :], ident_in).then_inc(consts, 16)

            def load_head(g, j):
                gg, s = g + j // GH, j % GH
                rows = bass.ds(gg * P + s * HD, HD)
                wait(sp, score_ready, MACROS * (4 * g + j - GH + 1))
                for part, (q_src, k_src) in enumerate(((q_hi, k_hi), (q_hi, k_lo), (q_lo, k_hi))):
                    at = slice(part * HD, (part + 1) * HD)
                    sp.dma_start(q_sb[at, s, :].bitcast(F32), q_src[rows, :]).then_inc(qk_in[s], 16)
                    sp.dma_start(k_sb[at, s, :].bitcast(F32), k_src[rows, :]).then_inc(qk_in[s], 16)
                sp.dma_start(k_sb[MASK_ROW:MASK_ROW + 1, s, :].bitcast(F32),
                             mask_b[bass.ds(gg, 1), :]).then_inc(qk_in[s], 16)
                wait(sp, vsq_ready, 2 * (4 * g + j - GH + 1))
                sp.dma_start(v_sb[:, s, :], v_t[bass.ds(gg * P, P), s * KT * HD:(s + 1) * KT * HD]
                             ).then_inc(v_in[s], 16)

            def load_maxrow(g, j):
                s = j % GH
                sp.wait_ge(rows_done, 4 * g + j + 1)
                for n in range(2):
                    sp.dma_start(q_sb[MAX_ROW + n:MAX_ROW + n + 1, s, :].bitcast(F32).rearrange(
                                     "a (t q) -> a t q", q=P),
                                 negmax_rows[n * KT:(n + 1) * KT, :].bitcast(F32)).then_inc(maxrow_in[s], 16)

            def regroup(g, j):
                jj = j % GH
                settled_wait(sp, pv_taken, 2 * (4 * g + j + 1))
                if jj == 0:
                    wait(sp, folded, 2 * (g + j // GH))
                for n, dst in enumerate((mean_a, sq_a, mean_b, sq_b)):
                    sp.dma_start(dst[jj * HD:(jj + 1) * HD, :], pv_sb[n * HD:(n + 1) * HD, j % 2, :]
                                 ).then_inc(regrouped[j % 2], 16)

            def sums_to_queries(f):
                sp.wait_ge(sums_taken, 2 * f + 2)
                sp.dma_start(sum_rows[bass.ds(f * GH, GH), :], sum_sb[0:P:HD, :]).then_inc(sums_stored, 16)
                sp.wait_ge(sums_stored, 16 * (f + 1))
                wait(sp, recipm_done, f)
                sp.dma_start(sum_c[:, :, :], sum_rows[bass.ds(f * GH, GH), :].rearrange(
                    "h (p e) -> p h e", p=P)).then_inc(sums_in, 16)
                sp.dma_start(mask_c[:, :], mask_f[bass.ds(f, 1), :].rearrange(
                    "a (p e) -> p (a e)", p=P)).then_inc(sums_in, 16)

            def recip_to_channels(f):
                sp.wait_ge(recipm_done, f + 1)
                sp.dma_start(recip_rows[bass.ds(f * GH, GH), :].rearrange("h (p e) -> p h e", p=P),
                             recip_m[:, :, :]).then_inc(recip_stored, 16)
                settled_wait(sp, recip_stored, 16 * (f + 1))
                wait(sp, scaled, 2 * f)
                for h in range(GH):
                    sp.dma_start(recip[h * HD:(h + 1) * HD, :],
                                 recip_rows[bass.ds(f * GH + h, 1), :].broadcast_to([HD, T])
                                 ).then_inc(recip_in, 16)

            def load_x(f):
                wait(sp, out_stored, 16 * f)
                sp.dma_start(x_sb[:, :], x_rows[bass.ds(f * P, P), :]).then_inc(x_in, 16)

            def store_out(f):
                sp.wait_ge(out_done, 2 * f + 2)
                sp.dma_start(out_rows[bass.ds(f * P, P), :], x_sb[:, :]).then_inc(out_stored, 16)

            sp.wait_ge(consts, 16 + 3)
            for j in range(3):
                load_head(0, j)
            load_maxrow(0, 0)

            def body(g):
                for j in range(GH):
                    if has_head(g, j + 1):
                        load_maxrow(g, j + 1)
                    if has_head(g, j + 3):
                        load_head(g, j + 3)
                    if j or exists(g - 1):
                        regroup(g if j else g - 1, j - 1 if j else GH - 1)
                    if j == 0 and exists(g - 1):
                        sums_to_queries(g - 1)
                    if j == 1 and exists(g - 1):
                        recip_to_channels(g - 1)
                    if j == 1 and exists(g - 2):
                        store_out(g - 2)
                    if j == 2 and exists(g - 1):
                        load_x(g - 1)

            over_groups(sp, body)
            regroup(LAST, GH - 1)
            sums_to_queries(LAST)
            recip_to_channels(LAST)
            store_out(LAST - 1)
            load_x(LAST)
            store_out(LAST)
            sp.wait_ge(out_stored, 16 * NG)

        @block.tensor
        def _(pe):
            pe.wait_ge(consts, 16 + 3)

            def max_tile(g, j, n, half):
                s = j % GH
                if n == 0 and half == 0:
                    pe.wait_ge(qk_in[s], 7 * 16 * (g + j // GH + 1))
                wait(pe, max_taken, 2 * KT * (4 * g + j) + 2 * n + half - 1)
                cols = slice(half * QH, (half + 1) * QH)
                pe.matmul(qk_max[:, cols], q_sb[0:MAX_ROW, s, n * P:(n + 1) * P],
                          k_sb[0:MAX_ROW, s, cols], start=True, stop=True).then_inc(max_ready, 1)

            def turn(g, j):
                pe.wait_ge(parts_done, 4 * g + j + 1)
                wait(pe, pv_taken, 2 * (4 * g + j - 1))
                pe.transpose(pv[0:2 * KT, 1, 0:P], negmax_parts[:, :], ident[:, :]).then_inc(turned, 1)

            def scores(g, j, m):
                if m == 0:
                    pe.wait_ge(maxrow_in[j], 32 * (g + 1))
                wait(pe, probs_ready, MACROS * (4 * g + j) + m - 1)
                for n in range(2):
                    kt = 2 * (m % 4) + n
                    mm = pe.matmul(score[:, m % 2, n * QH:(n + 1) * QH], k_sb[0:ROWS, j, kt * P:(kt + 1) * P],
                                   q_sb[0:ROWS, j, (m // 4) * QH:(m // 4 + 1) * QH], start=True, stop=True)
                mm.then_inc(score_ready, 1)

            def products(g, j, m):
                head, half = 4 * g + j, m // 4
                pe.wait_ge(probs_ready, MACROS * head + m + 1)
                if m == 0:
                    pe.wait_ge(vsq_ready, 2 * (head + 1))
                if m % 4 == 0:
                    wait(pe, pv_taken, 2 * head + half - 1)
                if m == 4 and has_head(g, j + 1):
                    pe.wait_ge(rows_done, head + 2)
                for n in range(2):
                    kt = 2 * (m % 4) + n
                    mm = pe.matmul(pv[64 * n:64 * n + 64, half, :], vv_sb[:, j, kt, :],
                                   probs[:, (2 * j + half) % 4, kt, :], start=(m % 4 == 0), stop=(m % 4 == 3))
                mm.then_inc(pv_done, 1)

            def sums(f, maxima):
                pe.wait_ge(totalled, 8 * f + 8)
                for half in range(2):
                    pe.wait_ge(max_taken, maxima - 1 + half)
                    for h in range(GH):
                        mm = pe.matmul(qk_max[h * HD:(h + 1) * HD, half * QH:(half + 1) * QH], ones[:, :],
                                       added[:, half, h, 0, :], start=True, stop=True)
                    mm.then_inc(sums_ready, 1)

            for n in range(KT):
                for half in range(2):
                    max_tile(0, 0, n, half)
            turn(0, 0)
            for n in range(KT):
                for half in range(2):
                    max_tile(0, 1, n, half)

            def body(g):
                for j in range(GH):
                    for m in range(MACROS):
                        scores(g, j, m)
                        with_sums = j == 0 and m == 4 and exists(g - 1)
                        if with_sums:
                            sums(g - 1, 2 * KT * (4 * g + 2) + 2 * m)
                            pe.wait_ge(sums_taken, 2 * g - 1)
                        if has_head(g, j + 2):
                            max_tile(g, j + 2, m, 0)
                        if m:
                            products(g, j, m - 1)
                        elif j:
                            products(g, j - 1, MACROS - 1)
                        elif exists(g - 1):
                            products(g - 1, GH - 1, MACROS - 1)
                        if m == 2 and has_head(g, j + 1):
                            turn(g, j + 1)
                        if with_sums:
                            pe.wait_ge(sums_taken, 2 * g)
                        if has_head(g, j + 2):
                            max_tile(g, j + 2, m, 1)

            over_groups(pe, body)
            products(LAST, GH - 1, MACROS - 1)
            sums(LAST, 2 * KT * (4 * LAST + 4))

        @block.scalar
        def _(act):
            def square_v(g, j):
                s = j % GH
                act.wait_ge(v_in[s], 16 * (g + j // GH + 1))
                wait(act, pv_done, MACROS * (4 * g + j - GH + 1))
                v = v_sb[:, s, :].rearrange("p (k d) -> p k d", d=HD)
                act.activation(vv_sb[:, s, :, 0:HD], v, ACT.Copy).then_inc(vsq_ready, 1)
                act.activation(vv_sb[:, s, :, HD:2 * HD], v, ACT.Square).then_inc(vsq_ready, 1)

            def exp(g, j, m):
                head, half = 4 * g + j, m // 4
                unit = 2 * head + half
                act.wait_ge(score_ready, MACROS * head + m + 1)
                if m % 4 == 0:
                    wait(act, all_added, unit - 3)
                kt = 2 * (m % 4)
                act.activation(probs[:, (2 * j + half) % 4, kt:kt + 2, :].rearrange("p k q -> p (k q)"),
                               score[:, m % 2, :], ACT.Exp, scale=SCALE).then_inc(probs_ready, 1)

            def take_pv(g, j, half):
                head = 4 * g + j
                act.wait_ge(pv_done, MACROS * head + 4 * half + 4)
                if half == 0:
                    wait(act, regrouped[j % 2], 64 * (2 * g + j // 2))
                act.activation(pv_sb[:, j % 2, half * QH:(half + 1) * QH], pv[:, half, :],
                               ACT.Copy).then_inc(pv_taken, 1)

            def mean_squared(f):
                act.wait_ge(scaled, 2 * f + 2)
                wait(act, prod_done, 2 * f)
                act.activation(std[:, :], mean[:, :], ACT.Square).then_inc(meansq_done, 1)

            def normalise(f):
                act.wait_ge(x_in, 16 * (f + 1))
                act.wait_ge(ab_done, 2 * (f + 1))
                act.activation(x_sb[:, :], x_sb[:, :], ACT.Identity, bias=ab[:, 1:2],
                               scale=ab[:, 0:1]).then_inc(xn_done, 1)

            def relu(f):
                act.wait_ge(var_done, 2 * (f + 1))
                act.activation(sq[:, :], sq[:, :], ACT.Relu).then_inc(relu_done, 1)

            def root(f):
                act.wait_ge(relu_done, f + 1)
                act.activation(std[:, :], sq[:, :], ACT.Sqrt).then_inc(std_done, 1)

            square_v(0, 0)

            def body(g):
                for j in range(GH):
                    for m in range(MACROS):
                        exp(g, j, m)
                        if m == 1 and j:
                            take_pv(g, j - 1, 1)
                        if m == 1 and not j and exists(g - 1):
                            take_pv(g - 1, GH - 1, 1)
                        if m == 5:
                            take_pv(g, j, 0)
                        if m == 6 and has_head(g, j + 1):
                            square_v(g, j + 1)
                        if j == 0 and m == 4 and exists(g - 2):
                            root(g - 2)
                        if j == 3 and m == 2 and exists(g - 1):
                            mean_squared(g - 1)
                        if j == 3 and m == 4 and exists(g - 1):
                            normalise(g - 1)
                        if j == 0 and m == 1 and exists(g - 2):
                            relu(g - 2)

            over_groups(act, body)
            take_pv(LAST, GH - 1, 1)
            relu(LAST - 1)
            root(LAST - 1)
            mean_squared(LAST)
            normalise(LAST)
            relu(LAST)
            root(LAST)

        @block.vector
        def _(dve):
            dve.memset(q_sb[MASK_ROW:ROWS, :, :].bitcast(F32), 1.0).then_inc(consts, 1)
            dve.memset(k_sb[MASK_ROW:ROWS, :, :].bitcast(F32), 1.0).then_inc(consts, 1)
            dve.memset(ones[:, :], 1.0).then_inc(consts, 1)

            def take_max(g, j, n, half):
                head = 4 * g + j
                dve.wait_ge(max_ready, 2 * KT * head + 2 * n + half + 1)
                if n == 0 and half == 0:
                    wait(dve, negmax_done, head - 1)
                dve.tensor_reduce(negmax2[:, j % 2, half, n:n + 1], qk_max[:, half * QH:(half + 1) * QH], AX_X,
                                  ALU.max, negate=True).then_inc(max_taken, 1)

            def split_max(g, j, step):
                head = 4 * g + j
                if step == 0:
                    settled_wait(dve, max_taken, 2 * KT * (head + 1))
                    wait(dve, parts_done, head)
                    dve.tensor_tensor(negmax[:, :], negmax2[:, j % 2, 0, :], negmax2[:, j % 2, 1, :],
                                      ALU.min).then_inc(negmax_done, 1)
                elif step == 1:
                    dve.wait_ge(negmax_done, head + 1)
                    wait(dve, turned, head)
                    dve.tensor_copy(negmax_parts[:, 0:KT].bitcast(F32R), negmax[:, :]).then_inc(parts_hi, 1)
                else:
                    dve.wait_ge(parts_hi, head + 1)
                    dve.tensor_tensor(negmax_parts[:, KT:2 * KT].bitcast(F32R), negmax[:, :],
                                      negmax_parts[:, 0:KT], ALU.subtract).then_inc(parts_done, 1)

            def take_rows(g, j):
                head = 4 * g + j
                dve.wait_ge(turned, head + 1)
                if j:
                    dve.wait_ge(maxrow_in[j - 1], 32 * (g + 1))
                dve.tensor_copy(negmax_rows[:, :], pv[0:2 * KT, 1, 0:P]).then_inc(rows_done, 1)

            def add_first(g, j, half, n):
                unit = 8 * g + 2 * j + half
                dve.wait_ge(pv_done, 4 * unit + 2)
                exps = probs[:, (2 * j + half) % 4, :, :]
                dve.tensor_tensor(exps[:, n, :], exps[:, n, :], exps[:, 2 + n, :], ALU.add).then_inc(first_added, 1)

            def take_sums(f):
                for half in range(2):
                    cols = slice(half * QH, (half + 1) * QH)
                    dve.wait_ge(sums_ready, 2 * f + half + 1)
                    wait(dve, sums_stored, 16 * f)
                    dve.tensor_copy(sum_sb[:, cols], qk_max[:, cols]).then_inc(sums_taken, 1)

            def invert(f):
                settled_wait(dve, sums_in, 32 * (f + 1))
                wait(dve, recipm_done, f)
                dve.reciprocal(recip_c[:, :, :], sum_c[:, :, :]).then_inc(recip_done, 1)
                settled_wait(dve, recip_done, f + 1)
                wait(dve, recip_stored, 16 * f)
                dve.tensor_tensor(recip_m[:, :, :], recip_c[:, :, :],
                                  mask_c[:, :].rearrange("p (a e) -> p a e", a=1).broadcast_to([P, GH, T // P]),
                                  ALU.mult).then_inc(recipm_done, 1)

            def take_ab(f):
                wait(dve, xn_done, f)
                for n in range(2):
                    dve.tensor_copy(ab[:, n:n + 1], norm_ab[:, n, bass.ds(f, 1)]).then_inc(ab_done, 1)

            def variance(f, half):
                cols = slice(half * QH, (half + 1) * QH)
                dve.wait_ge(meansq_done, f + 1)
                dve.tensor_tensor(sq[:, cols], sq[:, cols], std[:, cols], ALU.subtract).then_inc(var_done, 1)

            def times_std(f, half):
                cols = slice(half * QH, (half + 1) * QH)
                dve.wait_ge(std_done, f + 1)
                dve.wait_ge(xn_done, f + 1)
                dve.tensor_tensor(x_sb[:, cols], x_sb[:, cols], std[:, cols], ALU.mult).then_inc(prod_done, 1)

            def plus_mean(f, half):
                cols = slice(half * QH, (half + 1) * QH)
                dve.wait_ge(prod_done, 2 * f + half + 1)
                dve.tensor_tensor(x_sb[:, cols], x_sb[:, cols], mean[:, cols], ALU.add).then_inc(out_done, 1)

            for n in range(KT):
                for half in range(2):
                    take_max(0, 0, n, half)
            for step in range(3):
                split_max(0, 0, step)
            take_rows(0, 0)
            for n in range(KT):
                for half in range(2):
                    take_max(0, 1, n, half)

            def body(g):
                for j in range(GH):
                    for m in range(MACROS):
                        if j == 0 and m == 4 and exists(g - 1):
                            take_sums(g - 1)
                        for half in range(2):
                            if has_head(g, j + 1) and 2 * m + half < 3:
                                split_max(g, j + 1, 2 * m + half)
                            if has_head(g, j + 2):
                                take_max(g, j + 2, m, half)
                        if m == 2 and has_head(g, j + 1):
                            take_rows(g, j + 1)
                        if m == 3 or m == 4:
                            add_first(g, j, 0, m - 3)
                        if m == 7:
                            add_first(g, j, 1, 0)
                        if m == 0 and (j or exists(g - 1)):
                            add_first(g if j else g - 1, (j - 1) % GH, 1, 1)
                        if j == 0 and m in (5, 6) and exists(g - 2):
                            times_std(g - 2, m - 5)
                        if j == 1 and m in (1, 2) and exists(g - 2):
                            plus_mean(g - 2, m - 1)
                        if j == 1 and m == 5 and exists(g - 1):
                            invert(g - 1)
                            take_ab(g - 1)
                        if j == 3 and m in (5, 6) and exists(g - 1):
                            variance(g - 1, m - 5)

            over_groups(dve, body)
            add_first(LAST, GH - 1, 1, 1)
            for half in range(2):
                times_std(LAST - 1, half)
            for half in range(2):
                plus_mean(LAST - 1, half)
            take_sums(LAST)
            invert(LAST)
            take_ab(LAST)
            for half in range(2):
                variance(LAST, half)
            for half in range(2):
                times_std(LAST, half)
                plus_mean(LAST, half)

        @block.gpsimd
        def _(pool):
            def add_last(g, j, half):
                unit = 8 * g + 2 * j + half
                pool.wait_ge(pv_done, 4 * unit + 4)
                exps = probs[:, (2 * j + half) % 4, :, :].rearrange("p k q -> p (k q)")
                pool.tensor_tensor(exps[:, 4 * QH:6 * QH], exps[:, 4 * QH:6 * QH], exps[:, 6 * QH:8 * QH],
                                   ALU.add).then_inc(last_added, 1)
                pool.wait_ge(last_added, unit + 1)
                pool.wait_ge(first_added, 2 * unit + 2)
                if j == 0:
                    wait(pool, sums_ready, 2 * g)
                pool.tensor_tensor(added[:, half, j, :, :].rearrange("p k q -> p (k q)"), exps[:, 0:2 * QH],
                                   exps[:, 4 * QH:6 * QH], ALU.add).then_inc(all_added, 1)
                pool.wait_ge(all_added, unit + 1)
                pool.tensor_tensor(added[:, half, j, 0, :], added[:, half, j, 0, :], added[:, half, j, 1, :],
                                   ALU.add).then_inc(totalled, 1)

            def fold(f):
                for s in regrouped:
                    pool.wait_ge(s, 128 * (f + 1))
                wait(pool, scaled, 2 * f)
                pool.tensor_tensor(mean_raw[:, :], mean_a[:, :], mean_b[:, :], ALU.add).then_inc(folded, 1)
                pool.tensor_tensor(sq_raw[:, :], sq_a[:, :], sq_b[:, :], ALU.add).then_inc(folded, 1)

            def divide(f):
                pool.wait_ge(recip_in, 64 * (f + 1))
                pool.wait_ge(folded, 2 * (f + 1))
                wait(pool, out_done, 2 * f)
                pool.tensor_tensor(mean[:, :], mean_raw[:, :], recip[:, :], ALU.mult).then_inc(scaled, 1)
                pool.tensor_tensor(sq[:, :], sq_raw[:, :], recip[:, :], ALU.mult).then_inc(scaled, 1)

            def body(g):
                for j in range(GH):
                    if j:
                        add_last(g, j - 1, 1)
                    elif exists(g - 1):
                        add_last(g - 1, GH - 1, 1)
                    add_last(g, j, 0)
                    if j == 0 and exists(g - 1):
                        fold(g - 1)
                    if j == 2 and exists(g - 1):
                        divide(g - 1)

            over_groups(pool, body)
            add_last(LAST, GH - 1, 1)
            fold(LAST)
            divide(LAST)


def cross_attention(nc, x, kv, mask, wqT, bq, wkT, bk, wvT, bv, ident_in, out):
    B, C, T = x.shape
    groups = B * C // P

    def dram(name, shape):
        return nc.dram_tensor(name, shape, F32, kind="Internal").ap()

    scratch = [dram(n, (B * C, T)) for n in ("q_hi", "q_lo", "k_hi", "k_lo", "v_rows")]
    scratch += [dram(n, (groups, T)) for n in ("mask_rows", "mask_bias_rows")]
    sum_rows = dram("sum_rows", (groups * 4, T))
    recip_rows = dram("recip_rows", (groups * 4, T))
    with nc.sbuf_tensor("norm_ab", [P, 2, groups], F32) as norm_ab:
        project(nc, x, kv, mask, wqT, bq, wkT, bk, wvT, bv, scratch, norm_ab)
        attend(nc, x, out, ident_in, scratch, sum_rows, recip_rows, norm_ab)


def kernel(x, ctx_2048, mask_Bx1x2048_bf1, L0_xattn_Wq, L0_xattn_bq, L0_xattn_Wk, L0_xattn_bk, L0_xattn_Wv,
           L0_xattn_bv):
    import numpy as np
    import concourse.bacc as bacc
    from concourse.bass_utils import run_bass_kernel_spmd

    arrays = {
        "x": np.ascontiguousarray(x),
        "kv": np.ascontiguousarray(ctx_2048),
        "mask": np.ascontiguousarray(mask_Bx1x2048_bf1),
        "wq_t": np.ascontiguousarray(np.asarray(L0_xattn_Wq).T),
        "bq": np.ascontiguousarray(np.asarray(L0_xattn_bq).reshape(-1, P).T),
        "wk_t": np.ascontiguousarray(np.asarray(L0_xattn_Wk).T),
        "bk": np.ascontiguousarray(np.asarray(L0_xattn_bk).reshape(-1, P).T),
        "wv_t": np.ascontiguousarray(np.asarray(L0_xattn_Wv).T),
        "bv": np.ascontiguousarray(L0_xattn_bv),
        "identity": np.eye(P, dtype=np.float32),
    }
    nc = bacc.Bacc("TRN2", target_bir_lowering=False, num_devices=1)
    args = [nc.dram_tensor(n, a.shape, mybir.dt.from_np(a.dtype), kind="ExternalInput").ap()
            for n, a in arrays.items()]
    out = nc.dram_tensor("out", arrays["x"].shape, F32, kind="ExternalOutput").ap()
    cross_attention(nc, *args, out)
    return run_bass_kernel_spmd(nc, [arrays], core_ids=[0]).results[0]["out"]
```

```python
from contextlib import ExitStack

import concourse.bass as bass
from concourse import mybir

F32 = mybir.dt.float32
F32R = mybir.dt.float32r
U8 = mybir.dt.uint8
ALU = mybir.AluOpType
ACT = mybir.ActivationFunctionType
AX_X = mybir.AxisListType.X

P = 128
EPS = 1e-5
MASKED = 2.0 ** 127


def wait(eng, sem, value):
    if isinstance(value, int) and value <= 0:
        return
    eng.wait_ge(sem, value)


def settled_wait(eng, sem, value):
    wait(eng, sem, value)
    if not isinstance(value, int):
        eng.nop(nofuse=True)


class Maxima:
    HD = 32
    GH = P // HD
    QH = 512
    MASK_ROW, MAX_ROW, ROWS = 3 * HD, 3 * HD + 1, 3 * HD + 3
    MACROS = 8

    def __init__(self, nc, ctx, T, scratch):
        GH = self.GH
        self.KT = T // P
        self.scratch = scratch

        def sb(name, shape, dt):
            return ctx.enter_context(nc.sbuf_tensor(name, shape, dt))

        def psum(name, shape):
            return ctx.enter_context(nc.psum_tensor(name, shape, F32))

        def sem(name):
            return ctx.enter_context(nc.semaphore(name))

        self.q_sb = sb("q_sb", [P, GH, T], F32R)
        self.k_sb = sb("k_sb", [P, GH, T], F32R)
        self.negmax2 = sb("negmax2", [P, 2, 2, self.KT], F32)
        self.negmax = sb("negmax", [P, self.KT], F32)
        self.negmax_rows = sb("negmax_rows", [self.KT, 2, P], F32R)
        self.ones = sb("ones", [P, self.HD], F32)
        self.ident = sb("ident", [P, P], F32)
        self.qk_max = psum("qk_max", [P, 3, self.QH])
        self.pv = psum("pv", [P, 2, self.QH])

        self.ones_done = sem("ones_done")
        self.ident_in = sem("ident_in")
        self.qk_in = [sem(f"qk_in{i}") for i in range(GH)]
        self.maxrow_in = [sem(f"maxrow_in{i}") for i in range(GH)]
        self.max_ready = sem("max_ready")
        self.max_taken = sem("max_taken")
        self.negmax_done = sem("negmax_done")
        self.turned = sem("turned")
        self.rows_hi = sem("rows_hi")
        self.rows_done = sem("rows_done")
        self.score_ready = sem("score_ready")
        self.pv_taken = sem("pv_taken")

    def constants(self, pool):
        pool.memset(self.k_sb[self.MASK_ROW:self.ROWS, :, :].bitcast(F32), 1.0).then_inc(self.ones_done, 1)
        pool.wait_ge(self.ones_done, 1)
        pool.memset(self.q_sb[self.MASK_ROW:self.ROWS, :, :].bitcast(F32), 1.0).then_inc(self.ones_done, 1)
        pool.wait_ge(self.ones_done, 2)
        pool.memset(self.ones[:, :], 1.0).then_inc(self.ones_done, 1)

    def load_qk(self, sp, g, j):
        GH, HD = self.GH, self.HD
        q_hi, q_lo, k_hi, k_lo, v_t, mask_f, mask_b = self.scratch
        gg, s = g + j // GH, j % GH
        rows = bass.ds(gg * P + s * HD, HD)
        wait(sp, self.score_ready, 2 * self.MACROS * (4 * g + j - GH + 1))
        for part, (q_src, k_src) in enumerate(((q_hi, k_hi), (q_hi, k_lo), (q_lo, k_hi))):
            at = slice(part * HD, (part + 1) * HD)
            sp.dma_start(self.q_sb[at, s, :].bitcast(F32), q_src[rows, :]).then_inc(self.qk_in[s], 16)
            sp.dma_start(self.k_sb[at, s, :].bitcast(F32), k_src[rows, :]).then_inc(self.qk_in[s], 16)
        sp.dma_start(self.k_sb[self.MASK_ROW:self.MASK_ROW + 1, s, :].bitcast(F32),
                     mask_b[bass.ds(gg, 1), :]).then_inc(self.qk_in[s], 16)

    def load_maxrow(self, sp, g, j):
        s = j % self.GH
        sp.wait_ge(self.rows_done, 4 * g + j + 1)
        for n in range(2):
            sp.dma_start(self.q_sb[self.MAX_ROW + n:self.MAX_ROW + n + 1, s, :].bitcast(F32).rearrange(
                             "a (t q) -> a t q", q=P),
                         self.negmax_rows[:, n, :].bitcast(F32)
                         ).then_inc(self.maxrow_in[s], 16)

    def max_tile(self, pe, g, j, n, half):
        s = j % self.GH
        if n == 0 and half == 0:
            pe.wait_ge(self.qk_in[s], 7 * 16 * (g + j // self.GH + 1))
        i = 2 * self.KT * s + 2 * n + half
        wait(pe, self.max_taken, TILES_PER_GROUP * (g + j // self.GH) + before_in_bank(i) + 1)
        cols = slice(half * self.QH, (half + 1) * self.QH)
        pe.matmul(self.qk_max[:, bank_of(i), :], self.q_sb[0:self.MAX_ROW, s, n * P:(n + 1) * P],
                  self.k_sb[0:self.MAX_ROW, s, cols], start=True, stop=True).then_inc(self.max_ready, 1)

    def turn(self, pe, g, j):
        pe.wait_ge(self.negmax_done, 4 * g + j + 1)
        wait(pe, self.pv_taken, 2 * (4 * g + j - 1))
        pe.transpose(self.pv[0:self.KT, 1, 0:P], self.negmax[:, :], self.ident[:, :]).then_inc(self.turned, 1)

    def take_max(self, dve, g, j, n, half):
        head = 4 * g + j
        dve.wait_ge(self.max_ready, 2 * self.KT * head + 2 * n + half + 1)
        if n == 0 and half == 0:
            wait(dve, self.negmax_done, head - 1)
        bank = bank_of(2 * self.KT * (j % self.GH) + 2 * n + half)
        dve.tensor_reduce(self.negmax2[:, j % 2, half, n:n + 1], self.qk_max[:, bank, :], AX_X, ALU.max, negate=True).then_inc(self.max_taken, 1)

    def join_max(self, dve, g, j):
        head = 4 * g + j
        settled_wait(dve, self.max_taken, 2 * self.KT * (head + 1))
        wait(dve, self.turned, head)
        dve.tensor_reduce(self.negmax[:, :], self.negmax2[:, j % 2, :, :].rearrange("p h n -> p n h"), AX_X,
                          ALU.min).then_inc(self.negmax_done, 1)

    def take_rows(self, dve, g, j, part):
        head = 4 * g + j
        turned = self.pv[0:self.KT, 1, 0:P]
        if part == 0:
            dve.wait_ge(self.turned, head + 1)
            if j:
                dve.wait_ge(self.maxrow_in[j - 1], 32 * (g + 1))
            dve.tensor_copy(self.negmax_rows[:, 0, :], turned).then_inc(self.rows_hi, 1)
        else:
            dve.wait_ge(self.rows_hi, head + 1)
            dve.tensor_tensor(self.negmax_rows[:, 1, :], turned, self.negmax_rows[:, 0, :].bitcast(F32),
                              ALU.subtract).then_inc(self.rows_done, 1)


TILES_PER_GROUP = 64


def bank_of(i):
    return 1 if i == TILES_PER_GROUP - 1 else i % 3


def before_in_bank(i):
    at = i - 1
    while bank_of(at % TILES_PER_GROUP) != bank_of(i):
        at -= 1
    return at


def project(nc, x, kv, mask, wqT, bq, wkT, bk, wvT, bv, ident_in, scratch, norm_ab, mx):
    B, C, T = x.shape
    CT = C // P
    TT = T // P
    HALF = 512
    NH = T // HALF
    HD = 32
    HEADS = C // HD
    BANKS = 3
    TILES = CT * NH
    TPB = 2 * TILES + TT
    MAX0, JOIN0, TURN0, ROWS0, MAX1 = 2, 10, 11, 12, 12
    assert TPB % BANKS == 0 and CT == 4 and NH == 2
    q_hi, q_lo, k_hi, k_lo, v_t, mask_f, mask_b = scratch

    with ExitStack() as ctx:
        def sb(name, shape, dt):
            return ctx.enter_context(nc.sbuf_tensor(name, shape, dt))

        def sem(name):
            return ctx.enter_context(nc.semaphore(name))

        w_hi = sb("w_hi", [P, 3, CT, C], F32R)
        w_lo = sb("w_lo", [P, 3, CT, C], F32R)
        raw = sb("raw", [P, 4, T], F32)
        in_hi = sb("in_hi", [P, 2 * CT, T], F32R)
        in_lo = sb("in_lo", [P, 2 * CT, T], F32R)
        out_hi = sb("out_hi", [P, 2, T], F32R)
        out_lo = sb("out_lo", [P, 2, T], F32R)
        v_sb = sb("v_sb", [P, HEADS, TT, HD], F32)
        xm = sb("xm", [P, T], F32)
        mask_u8 = sb("mask_u8", [P, T], U8)
        mask_sb = sb("mask_sb", [P, T], F32)
        bqk = sb("bqk", [P, 2, CT], F32)
        bv_sb = sb("bv_sb", [P, C], F32)
        sum4 = sb("sum4", [P, CT], F32)
        sq4 = sb("sq4", [P, CT], F32)
        sums = sb("sums", [P, B * CT], F32)
        sqs = sb("sqs", [P, B * CT], F32)
        nval = sb("nval", [P, B], F32)
        rn = sb("rn", [P, B], F32)
        mean = sb("mean", [P, B * CT], F32)
        mean2 = sb("mean2", [P, B * CT], F32)
        var = sb("var", [P, B * CT], F32)
        mask_row = mx.k_sb[mx.MASK_ROW:mx.MASK_ROW + 1, mx.GH - 1, :]
        v_flat = v_sb[:, :, :, :].rearrange("p h t d -> p (h t d)")
        w_raw = [out_hi[:, :, :].bitcast(F32).rearrange("p s (c o) -> p (s c) o", o=C)]
        w_raw += [v_flat[:, i * CT * C:(i + 1) * CT * C].rearrange("p (c o) -> p c o", o=C) for i in range(2)]
        ps = [ctx.enter_context(nc.psum_tensor(f"proj{i}", [P, HALF], F32)) for i in range(BANKS)]

        w_in = [sem(f"w_in{i}") for i in range(3)]
        w_hi_done = sem("w_hi_done")
        w_lo_done = sem("w_lo_done")
        consts_in = sem("consts_in")
        raw_in = [sem(f"raw_in{i}") for i in range(4)]
        mask_in = sem("mask_in")
        hi_done = sem("hi_done")
        lo_done = sem("lo_done")
        mask_done = sem("mask_done")
        maskrow_done = sem("maskrow_done")
        nval_done = sem("nval_done")
        xm_done = sem("xm_done")
        sq_done = sem("sq_done")
        stat_done = sem("stat_done")
        mm_done = sem("mm_done")
        outhi_done = sem("outhi_done")
        evac_done = sem("evac_done")
        stored = [sem(f"stored{i}") for i in range(2)]
        v_stored = sem("v_stored")
        mask_stored = sem("mask_stored")
        chain = sem("chain")
        root = sem("root")

        block = ctx.enter_context(nc.Block())

        def over_batches(eng, body):
            body(0, first=True)
            with eng.Fori(1, B - 1) as b:
                body(b)
            body(B - 1, last=True)

        @block.sync
        def _(sp):
            def load_w(j, w):
                sp.dma_start(w_raw[j], w.rearrange("(c p) o -> p c o", p=P)).then_inc(w_in[j], 16)

            def load_x(b, r):
                wait(sp, lo_done, 8 * b - 3 + r)
                sp.dma_start(raw[:, r, :], channels(x, b, r)).then_inc(raw_in[r], 16)

            def load_kv(b, r):
                settled_wait(sp, lo_done, 8 * b + 1 + r)
                sp.wait_ge(xm_done, 4 * b + 1 + r)
                sp.dma_start(raw[:, r, :], channels(kv, b, r)).then_inc(raw_in[r], 16)

            def channels(src, b, r):
                if isinstance(b, int):
                    return src[b, r * P:(r + 1) * P, :]
                return src[bass.ds(b, 1), r * P:(r + 1) * P, :].rearrange("a p t -> (a p) t")

            def load_mask(b):
                settled_wait(sp, mask_done, b)
                row = mask[b] if isinstance(b, int) else mask[bass.ds(b, 1)].rearrange("a o t -> (a o) t")
                sp.dma_start(mask_u8[:, :], row.broadcast_to([P, T])).then_inc(mask_in, 16)

            def store_masks(b):
                sp.wait_ge(maskrow_done, b + 1)
                for g in range(CT):
                    sp.dma_start(mask_f[bass.ds(b * CT + g, 1), :], mask_sb[0:1, :]).then_inc(mask_stored, 16)
                    sp.dma_start(mask_b[bass.ds(b * CT + g, 1), :],
                                 mask_row.bitcast(F32)).then_inc(mask_stored, 16)

            def store(b, n, o):
                sp.wait_ge(evac_done, TPB * b + TILES * n + 2 * o + 2)
                rows = bass.ds(b * C + o * P, P)
                hi, lo = ((q_hi, q_lo), (k_hi, k_lo))[n]
                sp.dma_start(hi[rows, :], out_hi[:, o % 2, :].bitcast(F32)).then_inc(stored[o % 2], 16)
                sp.dma_start(lo[rows, :], out_lo[:, o % 2, :].bitcast(F32)).then_inc(stored[o % 2], 16)

            def store_v(b, part):
                sp.wait_ge(evac_done, TPB * b + 2 * TILES + (part + 1) * TT // 2)
                tiles = slice(part * TT // 2, (part + 1) * TT // 2)
                for g in range(CT):
                    sp.dma_start(v_t[bass.ds(b * C + g * P, P), :].rearrange(
                                     "p (h t d) -> p h t d", h=4, d=HD)[:, :, tiles, :],
                                 v_sb[:, 4 * g:4 * g + 4, tiles, :]).then_inc(v_stored, 16)

            load_mask(0)
            load_w(0, wqT)
            for r in range(CT):
                load_x(0, r)
            sp.dma_start(bqk[:, 0, :], bq).then_inc(consts_in, 16)
            sp.dma_start(bqk[:, 1, :], bk).then_inc(consts_in, 16)
            sp.dma_start(bv_sb[:, :], bv.rearrange("(a o) -> a o", a=1).broadcast_to([P, C])).then_inc(consts_in, 16)
            load_w(1, wkT)
            load_w(2, wvT)
            sp.dma_start(mx.ident[:, :], ident_in).then_inc(mx.ident_in, 16)

            def body(b, first=False, last=False):
                if last:
                    for s in stored:
                        sp.wait_ge(s, 4 * 32)
                    sp.wait_ge(mask_stored, B * CT * 32)
                    mx.load_qk(sp, 0, 0)
                for o in range(CT):
                    if first and o < 2:
                        load_kv(b, 2 * o)
                        load_kv(b, 2 * o + 1)
                    if first and o == 2:
                        store_masks(0)
                    if not last and o == 2:
                        load_mask(b + 1)
                    if not last and o == 3:
                        for r in range(CT):
                            load_x(b + 1, r)
                    store(b, 0, o)
                    if last and o < 2:
                        mx.load_qk(sp, 0, o + 1)
                for o in range(CT):
                    if not last and o == 3:
                        store_masks(b + 1)
                    store(b, 1, o)
                if last:
                    mx.load_maxrow(sp, 0, 0)
                else:
                    for r in range(CT):
                        load_kv(b + 1, r)
                for part in range(2):
                    store_v(b, part)

            over_batches(sp, body)
            for s in stored:
                sp.wait_ge(s, B * 4 * 32)
            sp.wait_ge(v_stored, B * CT * 32)
            sp.wait_ge(mask_stored, B * CT * 32)

        @block.gpsimd
        def _(pool):
            mx.constants(pool)

        @block.scalar
        def _(act):
            def weight_hi(j):
                act.wait_ge(w_in[j], 16)
                act.activation(w_hi[:, j, :, :], w_raw[j], ACT.Copy).then_inc(w_hi_done, 1)

            def part_hi(b, first, r):
                wait(act, mm_done, TPB * b - TPB + TILES if first == 0 else TPB * b)
                act.wait_ge(raw_in[r], 32 * b + (16 if first == 0 else 32))
                act.activation(in_hi[:, first + r, :], raw[:, r, :], ACT.Copy).then_inc(hi_done, 1)

            def square(b, r):
                act.wait_ge(xm_done, 4 * b + r + 1)
                if r == 0:
                    wait(act, stat_done, 2 * b)
                act.activation(xm[:, :], xm[:, :], ACT.Square, accum_out=sq4[:, r:r + 1]).then_inc(sq_done, 1)

            def evacuate_hi(b, n, i):
                o, half = i // NH, i % NH
                t = TILES * n + i
                act.wait_ge(mm_done, TPB * b + t + 1)
                if half == 0:
                    wait(act, stored[o % 2], 32 * (4 * b + 2 * n + o // 2))
                act.activation(out_hi[:, o % 2, half * HALF:(half + 1) * HALF], ps[t % BANKS][:, :],
                               ACT.Identity, bias=bqk[:, n, o:o + 1]).then_inc(outhi_done, 1)

            weight_hi(0)
            for r in range(CT):
                part_hi(0, 0, r)
            act.wait_ge(consts_in, 48)

            def body(b, first=False, last=False):
                for i in range(TILES):
                    evacuate_hi(b, 0, i)
                    if first and 1 <= i <= CT:
                        square(0, i - 1)
                    if first and i == CT - 1:
                        weight_hi(1)
                    if first and i in (CT, CT + 1):
                        part_hi(0, 4, 2 * (i - CT))
                        part_hi(0, 4, 2 * (i - CT) + 1)
                    if not first and i < CT:
                        part_hi(b, 4, i)
                for i in range(TILES):
                    evacuate_hi(b, 1, i)
                    if first and i == CT:
                        weight_hi(2)
                    if not last and i < CT:
                        part_hi(b + 1, 0, i)
                if last:
                    act.wait_ge(chain, 5)
                    act.activation(mean2[:, :], var[:, :], ACT.Sqrt).then_inc(root, 1)
                else:
                    for r in range(CT):
                        square(b + 1, r)

            over_batches(act, body)

        @block.vector
        def _(dve):
            def weight_lo(j):
                dve.wait_ge(w_hi_done, j + 1)
                dve.tensor_tensor(w_lo[:, j, :, :], w_raw[j], w_hi[:, j, :, :].bitcast(F32),
                                  ALU.subtract).then_inc(w_lo_done, 1)

            def take_mask(b):
                settled_wait(dve, mask_in, 16 * b + 16)
                settled_wait(dve, mask_stored, 32 * CT * b)
                wait(dve, xm_done, 4 * b)
                dve.tensor_copy(mask_sb[:, :], mask_u8[:, :]).then_inc(mask_done, 1)
                dve.wait_ge(mask_done, b + 1)
                dve.tensor_scalar(mask_row, mask_sb[mx.MASK_ROW:mx.MASK_ROW + 1, :], MASKED, -MASKED, ALU.mult,
                                  ALU.add).then_inc(maskrow_done, 1)
                dve.tensor_reduce(nval[:, bass.ds(b, 1)], mask_sb[:, :], AX_X, ALU.add).then_inc(nval_done, 1)

            def part_lo(b, first, r):
                dve.wait_ge(hi_done, 8 * b + first + r + 1)
                wait(dve, mm_done, TPB * b - TPB + TILES if first == 0 else TPB * b)
                dve.tensor_tensor(in_lo[:, first + r, :], raw[:, r, :], in_hi[:, first + r, :].bitcast(F32),
                                  ALU.subtract).then_inc(lo_done, 1)

            def times_mask(b, r):
                settled_wait(dve, sq_done, 4 * b + r)
                if r == 0:
                    wait(dve, stat_done, 2 * b)
                wait(dve, mask_done, b + 1)
                dve.tensor_tensor_reduce(xm[:, :], raw[:, r, :], mask_sb[:, :], 1.0, 0.0, ALU.mult,
                                         ALU.add, sum4[:, r:r + 1]).then_inc(xm_done, 1)

            def keep_sums(b):
                dve.wait_ge(xm_done, 4 * b + 4)
                dve.tensor_copy(sums[:, bass.ds(b * CT, CT)], sum4[:, :]).then_inc(stat_done, 1)
                settled_wait(dve, sq_done, 4 * b + 4)
                dve.tensor_copy(sqs[:, bass.ds(b * CT, CT)], sq4[:, :]).then_inc(stat_done, 1)

            def evacuate_lo(b, n, i):
                o, half = i // NH, i % NH
                t = TILES * n + i
                dve.wait_ge(outhi_done, 2 * TILES * b + t + 1)
                if half == 0:
                    wait(dve, stored[o % 2], 32 * (4 * b + 2 * n + o // 2))
                cols = slice(half * HALF, (half + 1) * HALF)
                dve.scalar_tensor_tensor(out_lo[:, o % 2, cols], ps[t % BANKS][:, :], bqk[:, n, o:o + 1],
                                         out_hi[:, o % 2, cols].bitcast(F32), ALU.add,
                                         ALU.subtract).then_inc(evac_done, 1)

            def evacuate_v(b, i):
                t = 2 * TILES + i
                settled_wait(dve, mm_done, TPB * b + t + 1)
                wait(dve, v_stored, 32 * CT * b)
                dve.tensor_tensor(v_sb[:, :, i, :], ps[t % BANKS][:, :].rearrange("p (h d) -> p h d", d=HD),
                                  bv_sb[:, :].rearrange("p (h d) -> p h d", d=HD),
                                  ALU.add).then_inc(evac_done, 1)

            def norm():
                dve.wait_ge(stat_done, 2 * B)
                dve.wait_ge(nval_done, B)
                dve.reciprocal(rn[:, :], nval[:, :]).then_inc(chain, 1)
                dve.wait_ge(chain, 1)
                by_batch = rn[:, :].rearrange("p (b o) -> p b o", o=1).broadcast_to([P, B, CT])

                def grouped(t):
                    return t[:, :].rearrange("p (b c) -> p b c", c=CT)

                dve.tensor_tensor(grouped(mean), grouped(sums), by_batch, ALU.mult).then_inc(chain, 1)
                dve.tensor_tensor(grouped(var), grouped(sqs), by_batch, ALU.mult).then_inc(chain, 1)
                dve.wait_ge(chain, 3)
                dve.tensor_tensor(mean2[:, :], mean[:, :], mean[:, :], ALU.mult).then_inc(chain, 1)
                dve.wait_ge(chain, 4)
                dve.tensor_tensor(sqs[:, :], var[:, :], mean2[:, :], ALU.subtract).then_inc(root, 1)
                dve.wait_ge(root, 1)
                dve.tensor_scalar(var[:, :], sqs[:, :], 0.0, EPS, ALU.max, ALU.add).then_inc(chain, 1)
                dve.wait_ge(root, 2)
                dve.reciprocal(norm_ab[:, 0, :], mean2[:, :]).then_inc(chain, 1)
                dve.wait_ge(chain, 6)
                dve.scalar_tensor_tensor(norm_ab[:, 1, :], mean[:, :], -1.0, norm_ab[:, 0, :], ALU.mult,
                                         ALU.mult).then_inc(chain, 1)
                dve.wait_ge(chain, 7)

            def first_heads(t):
                if MAX0 <= t < MAX0 + mx.KT:
                    for half in range(2):
                        mx.take_max(dve, 0, 0, t - MAX0, half)
                if t == JOIN0:
                    mx.join_max(dve, 0, 0)
                if t == ROWS0:
                    for part in range(2):
                        mx.take_rows(dve, 0, 0, part)
                if MAX1 <= t < MAX1 + mx.KT:
                    for half in range(2):
                        mx.take_max(dve, 0, 1, t - MAX1, half)

            dve.wait_ge(mx.ones_done, 1)
            take_mask(0)
            weight_lo(0)
            for r in range(CT):
                part_lo(0, 0, r)
            dve.wait_ge(consts_in, 48)

            def body(b, first=False, last=False):
                for i in range(TILES):
                    evacuate_lo(b, 0, i)
                    if first and i < CT:
                        times_mask(0, i)
                    if first and i == CT - 1:
                        weight_lo(1)
                    if first and i in (CT, CT + 1):
                        part_lo(0, 4, 2 * (i - CT))
                        part_lo(0, 4, 2 * (i - CT) + 1)
                    if not first and i < CT:
                        part_lo(b, 4, i)
                    if last:
                        first_heads(i)
                if first:
                    keep_sums(0)
                for i in range(TILES):
                    evacuate_lo(b, 1, i)
                    if first and i == CT + 2:
                        weight_lo(2)
                    if not last and i < CT:
                        part_lo(b + 1, 0, i)
                    if not last and i == CT:
                        take_mask(b + 1)
                    if last:
                        first_heads(TILES + i)
                for i in range(TT):
                    evacuate_v(b, i)
                    if not last and i < CT:
                        times_mask(b + 1, i)
                    if not last and i == CT:
                        keep_sums(b + 1)
                    if last:
                        first_heads(2 * TILES + i)
                    if last and i == CT:
                        norm()

            over_batches(dve, body)

        @block.tensor
        def _(pe):
            def products(b, t, pairs):
                wait(pe, evac_done, TPB * b + t - BANKS + 1)
                for n, (lhsT, rhs) in enumerate(pairs):
                    mm = pe.matmul(ps[t % BANKS][:, :], lhsT, rhs, start=(n == 0), stop=(n == len(pairs) - 1))
                mm.then_inc(mm_done, 1)

            def parts(a_hi, a_lo, b_hi, b_lo):
                return [(a_hi, b_hi), (a_hi, b_lo), (a_lo, b_hi)]

            def first_heads(t):
                if t == MAX0:
                    pe.wait_ge(mx.ones_done, 3)
                if MAX0 <= t < MAX0 + mx.KT:
                    for half in range(2):
                        mx.max_tile(pe, 0, 0, t - MAX0, half)
                if t == TURN0:
                    pe.wait_ge(mx.ident_in, 16)
                    mx.turn(pe, 0, 0)
                if MAX1 <= t < MAX1 + mx.KT:
                    for half in range(2):
                        mx.max_tile(pe, 0, 1, t - MAX1, half)

            def body(b, first=False, last=False):
                for n in range(2):
                    if first:
                        pe.wait_ge(w_lo_done, n + 1)
                    pe.wait_ge(lo_done, 8 * b + 4 + 4 * n)
                    for i in range(TILES):
                        out = slice((i // NH) * P, (i // NH + 1) * P)
                        cols = slice((i % NH) * HALF, (i % NH + 1) * HALF)
                        pairs = []
                        for c in range(CT):
                            pairs += parts(w_hi[:, n, c, out], w_lo[:, n, c, out],
                                           in_hi[:, 4 * n + c, cols], in_lo[:, 4 * n + c, cols])
                        products(b, TILES * n + i, pairs)
                        if last:
                            first_heads(TILES * n + i)
                if first:
                    pe.wait_ge(w_lo_done, 3)
                for i in range(TT):
                    rows = slice(i * P, (i + 1) * P)
                    pairs = []
                    for c in range(CT):
                        pairs += parts(in_hi[:, 4 + c, rows], in_lo[:, 4 + c, rows],
                                       w_hi[:, 2, c, :], w_lo[:, 2, c, :])
                    products(b, 2 * TILES + i, pairs)
                    if last:
                        first_heads(2 * TILES + i)

            over_batches(pe, body)


def attend(nc, x, out, scratch, sum_rows, recip_rows, norm_ab, mx):
    B, C, T = x.shape
    HD, GH, QH, MACROS, ROWS = mx.HD, mx.GH, mx.QH, mx.MACROS, mx.ROWS
    NG = B * C // P
    KT = T // P
    SCALE = float(HD) ** -0.5
    assert GH == 4 and KT == 8 and T == 2 * QH
    q_hi, q_lo, k_hi, k_lo, v_t, mask_f, mask_b = scratch
    x_rows = x.rearrange("b c t -> (b c) t")
    out_rows = out.rearrange("b c t -> (b c) t")

    with ExitStack() as ctx:
        def sb(name, shape, dt):
            return ctx.enter_context(nc.sbuf_tensor(name, shape, dt))

        def psum(name, shape):
            return ctx.enter_context(nc.psum_tensor(name, shape, F32))

        def sem(name):
            return ctx.enter_context(nc.semaphore(name))

        v_sb = sb("v_sb_", [P, GH, KT * HD], F32)
        vv_sb = sb("vv_sb", [P, GH, KT, 2 * HD], F32)
        probs = sb("probs", [P, 4, KT + 1, QH], F32)
        added = sb("added", [P, 2, GH, 2, QH], F32)
        pv_sb = sb("pv_sb", [P, 2, T], F32)
        mean_a = sb("mean_a", [P, T], F32)
        mean_b = sb("mean_b", [P, T], F32)
        sq_a = sb("sq_a", [P, T], F32)
        sq_b = sb("sq_b", [P, T], F32)
        mean_raw = sb("mean_raw", [P, T], F32)
        sq_raw = sb("sq_raw", [P, T], F32)
        mean = sb("mean_", [P, T], F32)
        sq = sb("sq", [P, T], F32)
        std = sb("std", [P, T], F32)
        x_sb = sb("x_sb", [P, T], F32)
        recip = sb("recip", [P, T], F32)
        sum_sb = sb("sum_sb", [P, T], F32)
        sum_c = sb("sum_c", [P, GH, T // P], F32)
        recip_c = sb("recip_c", [P, GH, T // P], F32)
        recip_m = sb("recip_m", [P, GH, T // P], F32)
        mask_c = sb("mask_c", [P, T // P], F32)
        ab = sb("ab", [P, 2], F32)
        score = psum("score", [P, 3, QH])
        q_sb, k_sb, qk_max, pv, ones = mx.q_sb, mx.k_sb, mx.qk_max, mx.pv, mx.ones
        max_taken, score_ready, pv_taken, maxrow_in = mx.max_taken, mx.score_ready, mx.pv_taken, mx.maxrow_in
        v_in = [sem(f"v_in{i}") for i in range(GH)]
        probs_ready = sem("probs_ready")
        vsq_ready = sem("vsq_ready")
        pv_done = sem("pv_done")
        first_added = sem("first_added")
        last_added = sem("last_added")
        all_added = sem("all_added")
        totalled = sem("totalled")
        regrouped = [sem(f"regrouped{i}") for i in range(2)]
        late_last = sem("late_last")
        late_all = sem("late_all")
        late_total = sem("late_total")
        sums_ready = sem("sums_ready")
        sums_taken = sem("sums_taken")
        sums_stored = sem("sums_stored")
        sums_in = sem("sums_in")
        recip_done = sem("recip_done")
        recipm_done = sem("recipm_done")
        recip_stored = sem("recip_stored")
        recip_in = sem("recip_in")
        folded = sem("folded")
        scaled = sem("scaled")
        meansq_done = sem("meansq_done")
        var_done = sem("var_done")
        relu_done = sem("relu_done")
        std_done = sem("std_done")
        x_in = sem("x_in")
        ab_done = sem("ab_done")
        xn_done = sem("xn_done")
        prod_done = sem("prod_done")
        out_done = sem("out_done")
        out_stored = sem("out_stored")

        block = ctx.enter_context(nc.Block())
        LAST = NG - 1
        SUMS_AT = MACROS - 2
        SUM_TILE = [2 * KT * 2 + 2 * m for m in (SUMS_AT, SUMS_AT + 1)]
        SUM_BANK = [bank_of(i) for i in SUM_TILE]
        LATE = 2

        def over_groups(eng, body):
            for g in range(3):
                body(g)
            with eng.Fori(3, LAST) as g:
                body(g)
            body(LAST)

        def is_last(g):
            return isinstance(g, int) and g == LAST

        def exists(f):
            return not isinstance(f, int) or f >= 0

        def has_head(g, j):
            return not (is_last(g) and j >= GH)

        @block.sync
        def _(sp):
            def load_v(g, j):
                gg, s = g + j // GH, j % GH
                wait(sp, vsq_ready, 2 * (4 * g + j - GH + 1))
                sp.dma_start(v_sb[:, s, :], v_t[bass.ds(gg * P, P), s * KT * HD:(s + 1) * KT * HD]
                             ).then_inc(v_in[s], 16)

            def regroup(g, j):
                jj = j % GH
                settled_wait(sp, pv_taken, 2 * (4 * g + j + 1))
                if jj == 0:
                    wait(sp, folded, 2 * (g + j // GH))
                for n, dst in enumerate((mean_a, sq_a, mean_b, sq_b)):
                    sp.dma_start(dst[jj * HD:(jj + 1) * HD, :], pv_sb[n * HD:(n + 1) * HD, j % 2, :]
                                 ).then_inc(regrouped[j % 2], 16)

            def sums_to_queries(f):
                sp.wait_ge(sums_taken, 2 * f + 2)
                sp.dma_start(sum_rows[bass.ds(f * GH, GH), :], sum_sb[0:P:HD, :]).then_inc(sums_stored, 16)
                sp.wait_ge(sums_stored, 16 * (f + 1))
                wait(sp, recipm_done, f)
                sp.dma_start(sum_c[:, :, :], sum_rows[bass.ds(f * GH, GH), :].rearrange(
                    "h (p e) -> p h e", p=P)).then_inc(sums_in, 16)
                sp.dma_start(mask_c[:, :], mask_f[bass.ds(f, 1), :].rearrange(
                    "a (p e) -> p (a e)", p=P)).then_inc(sums_in, 16)

            def recip_to_channels(f):
                sp.wait_ge(recipm_done, f + 1)
                sp.dma_start(recip_rows[bass.ds(f * GH, GH), :].rearrange("h (p e) -> p h e", p=P),
                             recip_m[:, :, :]).then_inc(recip_stored, 16)
                settled_wait(sp, recip_stored, 16 * (f + 1))
                wait(sp, scaled, 2 * f)
                for h in range(GH):
                    sp.dma_start(recip[h * HD:(h + 1) * HD, :],
                                 recip_rows[bass.ds(f * GH + h, 1), :].broadcast_to([HD, T])
                                 ).then_inc(recip_in, 16)

            def load_x(f):
                wait(sp, out_stored, 16 * f)
                sp.dma_start(x_sb[:, :], x_rows[bass.ds(f * P, P), :]).then_inc(x_in, 16)

            def store_out(f):
                sp.wait_ge(out_done, 2 * f + 2)
                sp.dma_start(out_rows[bass.ds(f * P, P), :], x_sb[:, :]).then_inc(out_stored, 16)

            for j in range(3):
                load_v(0, j)

            def body(g):
                for j in range(GH):
                    if has_head(g, j + 1):
                        mx.load_maxrow(sp, g, j + 1)
                    if has_head(g, j + 3):
                        mx.load_qk(sp, g, j + 3)
                        load_v(g, j + 3)
                    if j or exists(g - 1):
                        regroup(g if j else g - 1, j - 1 if j else GH - 1)
                    if j == 0 and exists(g - 1):
                        sums_to_queries(g - 1)
                    if j == 2 and exists(g - 1):
                        recip_to_channels(g - 1)
                    if j == 3 and exists(g - 2):
                        store_out(g - 2)
                    if j == 3 and exists(g - 1):
                        load_x(g - 1)

            over_groups(sp, body)
            regroup(LAST, GH - 1)
            sums_to_queries(LAST)
            store_out(LAST - 1)
            recip_to_channels(LAST)
            load_x(LAST)
            store_out(LAST)
            sp.wait_ge(out_stored, 16 * NG)

        @block.tensor
        def _(pe):
            def scores(g, j, m):
                if m == 0:
                    pe.wait_ge(maxrow_in[j], 32 * (g + 1))
                for n in range(2):
                    i = 2 * MACROS * j + 2 * m + n
                    wait(pe, probs_ready, TILES_PER_GROUP * g + before_in_bank(i) + 1)
                    kt = 2 * (m % 4) + n
                    pe.matmul(score[:, bank_of(i), :], k_sb[0:ROWS, j, kt * P:(kt + 1) * P],
                              q_sb[0:ROWS, j, (m // 4) * QH:(m // 4 + 1) * QH], start=True, stop=True
                              ).then_inc(score_ready, 1)

            def products(g, j, m):
                head, half = 4 * g + j, m // 4
                pe.wait_ge(probs_ready, 2 * MACROS * head + 2 * m + 2)
                if m == 0:
                    pe.wait_ge(vsq_ready, 2 * (head + 1))
                if m % 4 == 0:
                    wait(pe, pv_taken, 2 * head + half - 1)
                if m == 4 and has_head(g, j + 1):
                    pe.wait_ge(mx.rows_done, head + 2)
                for n in range(2):
                    kt = 2 * (m % 4) + n
                    mm = pe.matmul(pv[64 * n:64 * n + 64, half, :], vv_sb[:, j, kt, :],
                                   probs[:, (2 * j + half) % 4, kt, :], start=(m % 4 == 0), stop=(m % 4 == 3))
                mm.then_inc(pv_done, 1)

            def sums(f, half, maxima):
                if half == 0:
                    late = 2 * (GH - LATE) if is_last(f) else 0
                    pe.wait_ge(totalled, 8 * f + 8 - late)
                    wait(pe, late_total, late)
                pe.wait_ge(max_taken, maxima)
                for h in range(GH):
                    mm = pe.matmul(qk_max[h * HD:(h + 1) * HD, SUM_BANK[half], :], ones[:, :],
                                   added[:, half, h, 0, :], start=True, stop=True)
                mm.then_inc(sums_ready, 1)

            def body(g):
                for j in range(GH):
                    for m in range(MACROS):
                        scores(g, j, m)
                        with_sums = j == 0 and m >= SUMS_AT and exists(g - 1)
                        if with_sums:
                            sums(g - 1, m - SUMS_AT, TILES_PER_GROUP * g + before_in_bank(SUM_TILE[m - SUMS_AT]) + 1)
                        elif has_head(g, j + 2):
                            mx.max_tile(pe, g, j + 2, m, 0)
                        if m:
                            products(g, j, m - 1)
                        elif j:
                            products(g, j - 1, MACROS - 1)
                        elif exists(g - 1):
                            products(g - 1, GH - 1, MACROS - 1)
                        if m == 2 and has_head(g, j + 1):
                            mx.turn(pe, g, j + 1)
                        if with_sums:
                            pe.wait_ge(sums_taken, 2 * g - 1 + m - SUMS_AT)
                            mx.max_tile(pe, g, j + 2, m, 0)
                        if has_head(g, j + 2):
                            mx.max_tile(pe, g, j + 2, m, 1)

            over_groups(pe, body)
            products(LAST, GH - 1, MACROS - 1)
            for half in range(2):
                sums(LAST, half, TILES_PER_GROUP * NG)

        @block.scalar
        def _(act):
            def square_v(g, j):
                s = j % GH
                act.wait_ge(v_in[s], 16 * (g + j // GH + 1))
                wait(act, pv_done, MACROS * (4 * g + j - GH + 1))
                v = v_sb[:, s, :].rearrange("p (k d) -> p k d", d=HD)
                act.activation(vv_sb[:, s, :, 0:HD], v, ACT.Copy).then_inc(vsq_ready, 1)
                act.activation(vv_sb[:, s, :, HD:2 * HD], v, ACT.Square).then_inc(vsq_ready, 1)

            def exp(g, j, m):
                head, half = 4 * g + j, m // 4
                unit = 2 * head + half
                if m % 4 == 0:
                    wait(act, all_added, unit - 3)
                for n in range(2):
                    act.wait_ge(score_ready, 2 * MACROS * head + 2 * m + n + 1)
                    act.activation(probs[:, (2 * j + half) % 4, 2 * (m % 4) + n, :],
                                   score[:, bank_of(2 * MACROS * j + 2 * m + n), :], ACT.Exp, scale=SCALE
                                   ).then_inc(probs_ready, 1)

            def take_pv(g, j, half):
                head = 4 * g + j
                act.wait_ge(pv_done, MACROS * head + 4 * half + 4)
                if half == 0:
                    wait(act, regrouped[j % 2], 64 * (2 * g + j // 2))
                act.activation(pv_sb[:, j % 2, half * QH:(half + 1) * QH], pv[:, half, :],
                               ACT.Copy).then_inc(pv_taken, 1)

            def mean_squared(f):
                act.wait_ge(scaled, 2 * f + (1 if is_last(f) else 2))
                wait(act, prod_done, 2 * f)
                act.activation(std[:, :], mean[:, :], ACT.Square).then_inc(meansq_done, 1)

            def normalise(f):
                act.wait_ge(x_in, 16 * (f + 1))
                act.wait_ge(ab_done, 2 * (f + 1))
                act.activation(x_sb[:, :], x_sb[:, :], ACT.Identity, bias=ab[:, 1:2],
                               scale=ab[:, 0:1]).then_inc(xn_done, 1)

            def relu(f):
                act.wait_ge(var_done, f + 1)
                act.activation(sq[:, :], sq[:, :], ACT.Relu).then_inc(relu_done, 1)

            def root(f):
                act.wait_ge(relu_done, f + 1)
                act.activation(std[:, :], sq[:, :], ACT.Sqrt).then_inc(std_done, 1)

            square_v(0, 0)

            def body(g):
                for j in range(GH):
                    for m in range(MACROS):
                        exp(g, j, m)
                        if m == 1 and j:
                            take_pv(g, j - 1, 1)
                        if m == 1 and not j and exists(g - 1):
                            take_pv(g - 1, GH - 1, 1)
                        if m == 5:
                            take_pv(g, j, 0)
                        if m == 6 and has_head(g, j + 1):
                            square_v(g, j + 1)
                        if j == 0 and m == 7 and exists(g - 2):
                            root(g - 2)
                        if j == 0 and m == 0 and exists(g - 2):
                            mean_squared(g - 2)
                        if j == 0 and m == 4 and exists(g - 2):
                            normalise(g - 2)
                        if j == 0 and m == 6 and exists(g - 2):
                            relu(g - 2)

            over_groups(act, body)
            take_pv(LAST, GH - 1, 1)
            mean_squared(LAST - 1)
            normalise(LAST - 1)
            relu(LAST - 1)
            root(LAST - 1)
            mean_squared(LAST)
            normalise(LAST)
            relu(LAST)
            root(LAST)

        @block.vector
        def _(dve):
            def add_first(g, j, half, n):
                unit = 8 * g + 2 * j + half
                dve.wait_ge(pv_done, 4 * unit + 2)
                exps = probs[:, (2 * j + half) % 4, :, n * QH // 4:(n + 1) * QH // 4]
                dve.tensor_reduce(exps[:, KT, :], exps[:, 0:3, :].rearrange("p k q -> p q k"), AX_X,
                                  ALU.add).then_inc(first_added, 1)

            def add_late(j, half):
                done = 2 * (j - LATE) + half
                dve.wait_ge(pv_done, 4 * (8 * LAST + 2 * j + half) + 4)
                exps = probs[:, (2 * j + half) % 4, :, :]
                dve.tensor_tensor(exps[:, 3:5, :], exps[:, 3:5, :], exps[:, 5:7, :], ALU.add).then_inc(late_last, 1)
                dve.wait_ge(late_last, done + 1)
                dve.wait_ge(first_added, 4 * (8 * LAST + 2 * j + half) + 4)
                dve.tensor_tensor(added[:, half, j, :, :], exps[:, 3:5, :], exps[:, KT - 1:KT + 1, :],
                                  ALU.add).then_inc(late_all, 1)
                dve.wait_ge(late_all, done + 1)
                dve.tensor_tensor(added[:, half, j, 0, :], added[:, half, j, 0, :], added[:, half, j, 1, :],
                                  ALU.add).then_inc(late_total, 1)

            def take_sums(f, half):
                cols = slice(half * QH, (half + 1) * QH)
                dve.wait_ge(sums_ready, 2 * f + half + 1)
                wait(dve, sums_stored, 16 * f)
                dve.tensor_copy(sum_sb[:, cols], qk_max[:, SUM_BANK[half], :]).then_inc(sums_taken, 1)

            def invert(f):
                settled_wait(dve, sums_in, 32 * (f + 1))
                wait(dve, recipm_done, f)
                dve.reciprocal(recip_c[:, :, :], sum_c[:, :, :]).then_inc(recip_done, 1)
                settled_wait(dve, recip_done, f + 1)
                wait(dve, recip_stored, 16 * f)
                dve.tensor_tensor(recip_m[:, :, :], recip_c[:, :, :],
                                  mask_c[:, :].rearrange("p (a e) -> p a e", a=1).broadcast_to([P, GH, T // P]),
                                  ALU.mult).then_inc(recipm_done, 1)

            def take_ab(f):
                wait(dve, xn_done, f)
                for n in range(2):
                    dve.tensor_copy(ab[:, n:n + 1], norm_ab[:, n, bass.ds(f, 1)]).then_inc(ab_done, 1)

            def times_std(f, half):
                cols = slice(half * QH, (half + 1) * QH)
                dve.wait_ge(std_done, f + 1)
                dve.wait_ge(xn_done, f + 1)
                dve.tensor_tensor(x_sb[:, cols], x_sb[:, cols], std[:, cols], ALU.mult).then_inc(prod_done, 1)

            def plus_mean(f, half):
                cols = slice(half * QH, (half + 1) * QH)
                dve.wait_ge(prod_done, 2 * f + half + 1)
                dve.tensor_tensor(x_sb[:, cols], x_sb[:, cols], mean[:, cols], ALU.add).then_inc(out_done, 1)

            def body(g):
                for j in range(GH):
                    for m in range(MACROS):
                        for half in range(2):
                            if j == 0 and m >= SUMS_AT and half == 0 and exists(g - 1):
                                take_sums(g - 1, m - SUMS_AT)
                            if has_head(g, j + 1) and m == 0 and half == 1:
                                mx.join_max(dve, g, j + 1)
                            if has_head(g, j + 2):
                                mx.take_max(dve, g, j + 2, m, half)
                            if has_head(g, j + 1) and m == 2:
                                mx.take_rows(dve, g, j + 1, half)
                        if m >= 2 and m < 6:
                            add_first(g, j, 0, m - 2)
                        if m >= 6:
                            add_first(g, j, 1, m - 6)
                        if m < 2 and (j or exists(g - 1)):
                            add_first(g if j else g - 1, (j - 1) % GH, 1, m + 2)
                        if is_last(g) and j >= LATE and m == 5:
                            add_late(j, 0)
                        if is_last(g) and j > LATE and m == 1:
                            add_late(j - 1, 1)
                        if j == 1 and m in (3, 6) and exists(g - 2):
                            times_std(g - 2, m // 6)
                        if j == 2 and m == 1 and exists(g - 1):
                            invert(g - 1)
                            take_ab(g - 1)
                        if j == 2 and m in (4, 7) and exists(g - 2):
                            plus_mean(g - 2, m // 7)

            over_groups(dve, body)
            for n in range(2, 4):
                add_first(LAST, GH - 1, 1, n)
            add_late(GH - 1, 1)
            for half in range(2):
                take_sums(LAST, half)
            for half in range(2):
                times_std(LAST - 1, half)
            for half in range(2):
                plus_mean(LAST - 1, half)
            invert(LAST)
            take_ab(LAST)
            dve.wait_ge(recip_in, 64 * (LAST + 1))
            dve.wait_ge(folded, 2 * (LAST + 1))
            dve.tensor_tensor(mean[:, :], mean_raw[:, :], recip[:, :], ALU.mult).then_inc(scaled, 1)
            dve.tensor_tensor(sq[:, :], sq_raw[:, :], recip[:, :], ALU.mult).then_inc(scaled, 1)
            dve.wait_ge(meansq_done, LAST + 1)
            dve.wait_ge(scaled, 2 * LAST + 2)
            dve.tensor_tensor(sq[:, :], sq[:, :], std[:, :], ALU.subtract).then_inc(var_done, 1)
            for half in range(2):
                times_std(LAST, half)
                plus_mean(LAST, half)

        @block.gpsimd
        def _(pool):
            def add_last(g, j, half):
                unit = 8 * g + 2 * j + half
                pool.wait_ge(pv_done, 4 * unit + 4)
                exps = probs[:, (2 * j + half) % 4, :, :]
                pool.tensor_tensor(exps[:, 3:5, :], exps[:, 3:5, :], exps[:, 5:7, :], ALU.add).then_inc(last_added, 1)
                pool.wait_ge(last_added, unit + 1)
                pool.wait_ge(first_added, 4 * unit + 4)
                if j == 0:
                    wait(pool, sums_ready, 2 * g)
                pool.tensor_tensor(added[:, half, j, :, :], exps[:, 3:5, :], exps[:, KT - 1:KT + 1, :],
                                   ALU.add).then_inc(all_added, 1)
                pool.wait_ge(all_added, unit + 1)
                pool.tensor_tensor(added[:, half, j, 0, :], added[:, half, j, 0, :], added[:, half, j, 1, :],
                                   ALU.add).then_inc(totalled, 1)

            def fold(f):
                for s in regrouped:
                    pool.wait_ge(s, 128 * (f + 1))
                wait(pool, scaled, 2 * f)
                pool.tensor_tensor(mean_raw[:, :], mean_a[:, :], mean_b[:, :], ALU.add).then_inc(folded, 1)
                pool.tensor_tensor(sq_raw[:, :], sq_a[:, :], sq_b[:, :], ALU.add).then_inc(folded, 1)

            def divide(f):
                pool.wait_ge(recip_in, 64 * (f + 1))
                pool.wait_ge(folded, 2 * (f + 1))
                wait(pool, out_done, 2 * f)
                pool.tensor_tensor(mean[:, :], mean_raw[:, :], recip[:, :], ALU.mult).then_inc(scaled, 1)
                pool.tensor_tensor(sq[:, :], sq_raw[:, :], recip[:, :], ALU.mult).then_inc(scaled, 1)

            def variance(f):
                pool.wait_ge(meansq_done, f + 1)
                pool.tensor_tensor(sq[:, :], sq[:, :], std[:, :], ALU.subtract).then_inc(var_done, 1)

            def body(g):
                for j in range(GH):
                    late = is_last(g) and j >= LATE
                    if j == 0 and exists(g - 1):
                        add_last(g - 1, GH - 1, 1)
                    if j and not (late and j > LATE):
                        add_last(g, j - 1, 1)
                    if j == 0 and exists(g - 2):
                        variance(g - 2)
                    if j == 0 and exists(g - 1):
                        fold(g - 1)
                    if j == 3 and exists(g - 1):
                        divide(g - 1)
                    if not late:
                        add_last(g, j, 0)

            over_groups(pool, body)
            variance(LAST - 1)
            fold(LAST)


def cross_attention(nc, x, kv, mask, wqT, bq, wkT, bk, wvT, bv, ident_in, out):
    B, C, T = x.shape
    groups = B * C // P

    def dram(name, shape):
        return nc.dram_tensor(name, shape, F32, kind="Internal").ap()

    scratch = [dram(n, (B * C, T)) for n in ("q_hi", "q_lo", "k_hi", "k_lo", "v_rows")]
    scratch += [dram(n, (groups, T)) for n in ("mask_rows", "mask_bias_rows")]
    sum_rows = dram("sum_rows", (groups * 4, T))
    recip_rows = dram("recip_rows", (groups * 4, T))
    with ExitStack() as ctx:
        norm_ab = ctx.enter_context(nc.sbuf_tensor("norm_ab", [P, 2, groups], F32))
        mx = Maxima(nc, ctx, T, scratch)
        project(nc, x, kv, mask, wqT, bq, wkT, bk, wvT, bv, ident_in, scratch, norm_ab, mx)
        attend(nc, x, out, scratch, sum_rows, recip_rows, norm_ab, mx)


def kernel(x, ctx_2048, mask_Bx1x2048_bf1, L0_xattn_Wq, L0_xattn_bq, L0_xattn_Wk, L0_xattn_bk, L0_xattn_Wv,
           L0_xattn_bv):
    import numpy as np
    import concourse.bacc as bacc
    from concourse.bass_utils import run_bass_kernel_spmd

    arrays = {
        "x": np.ascontiguousarray(x),
        "kv": np.ascontiguousarray(ctx_2048),
        "mask": np.ascontiguousarray(mask_Bx1x2048_bf1),
        "wq_t": np.ascontiguousarray(np.asarray(L0_xattn_Wq).T),
        "bq": np.ascontiguousarray(np.asarray(L0_xattn_bq).reshape(-1, P).T),
        "wk_t": np.ascontiguousarray(np.asarray(L0_xattn_Wk).T),
        "bk": np.ascontiguousarray(np.asarray(L0_xattn_bk).reshape(-1, P).T),
        "wv_t": np.ascontiguousarray(np.asarray(L0_xattn_Wv).T),
        "bv": np.ascontiguousarray(L0_xattn_bv),
        "identity": np.eye(P, dtype=np.float32),
    }
    nc = bacc.Bacc("TRN2", target_bir_lowering=False, num_devices=1)
    args = [nc.dram_tensor(n, a.shape, mybir.dt.from_np(a.dtype), kind="ExternalInput").ap()
            for n, a in arrays.items()]
    out = nc.dram_tensor("out", arrays["x"].shape, F32, kind="ExternalOutput").ap()
    cross_attention(nc, *args, out)
    return run_bass_kernel_spmd(nc, [arrays], core_ids=[0]).results[0]["out"]
```
